# Optimizing a Trainium2 kernel written in Bass

```python
import numpy as np
import jax
import jax.numpy as jnp

def _softmax(x, axis=-1):
    return jax.nn.softmax(x, axis=axis)

def _gelu(x):
    return jax.nn.gelu(x, approximate=True)

def _silu(x):
    return jax.nn.silu(x)

def _sigmoid(x):
    return jax.nn.sigmoid(x)

def _layernorm(x, axis=-1, eps=1e-05):
    m = jnp.mean(x, axis=axis, keepdims=True)
    v = jnp.var(x, axis=axis, keepdims=True)
    return (x - m) / jnp.sqrt(v + eps)

def _scatter_add(tgt, idx, src, axis=0):
    return tgt.at[idx].add(src)

def _segment_sum(src, seg, n):
    return jax.ops.segment_sum(src, seg, n)
kernel_name = 'mk_seq_postln_d1_jaxref_r8_d0f9a2'

def setup_inputs(seed: int=0):
    np.random.seed(seed)
    _w = jnp.asarray

    def _L0_attn_setup():
        import jax, jax.numpy as jnp
        import numpy as np
        B, K, D = (8, 256, 128)
        INNER = 2 * D
        EPS = 1e-05

        def _silu(x):
            return x * jax.nn.sigmoid(x)
        key = jax.random.key(seed)
        k0, k1, k2, k3 = jax.random.split(key, 4)
        s_in = 1.0 / np.sqrt(D)
        s_inner = 1.0 / np.sqrt(INNER)
        return {'x': jax.random.normal(k0, (B, K, D), dtype=jnp.float32), 'w_norm': jnp.ones((D,), dtype=jnp.float32), 'W_in': (jax.random.normal(k1, (2 * INNER, D)) * s_in).astype(jnp.float32), 'W_dt': (jax.random.normal(k2, (INNER, INNER)) * s_inner).astype(jnp.float32), 'b_dt': jnp.zeros((INNER,), dtype=jnp.float32), 'W_out': (jax.random.normal(k3, (D, INNER)) * s_inner).astype(jnp.float32)}
    _L0_attn_in = _L0_attn_setup()

    def _L0_ffn_setup():
        import jax, jax.numpy as jnp
        import numpy as np

        def _binarize(w):
            alpha = jax.lax.stop_gradient(jnp.mean(jnp.abs(w), axis=1, keepdims=True))
            bw = alpha * jnp.sign(w)
            return w + jax.lax.stop_gradient(bw - w)
        key = jax.random.key(seed)
        k1, k2, k3, k4, k5 = jax.random.split(key, 5)
        D, H = (128, 512)
        x = jax.random.normal(k1, (64, 196, D), dtype=jnp.float32)
        w1 = jax.random.normal(k2, (H, D), dtype=jnp.float32) * 0.02
        b1 = jax.random.normal(k3, (H,), dtype=jnp.float32) * 0.02
        w2 = jax.random.normal(k4, (D, H), dtype=jnp.float32) * 0.02
        b2 = jax.random.normal(k5, (D,), dtype=jnp.float32) * 0.02
        return {'x': x, 'w1': w1, 'b1': b1, 'w2': w2, 'b2': b2}
    _L0_ffn_in = _L0_ffn_setup()
    _d = {'L0_attn_x': _L0_attn_in['x'], 'L0_attn_w_norm': _L0_attn_in['w_norm'], 'L0_attn_W_in': _L0_attn_in['W_in'], 'L0_attn_W_dt': _L0_attn_in['W_dt'], 'L0_attn_b_dt': _L0_attn_in['b_dt'], 'L0_attn_W_out': _L0_attn_in['W_out'], 'L0_ffn_w1': _L0_ffn_in['w1'], 'L0_ffn_b1': _L0_ffn_in['b1'], 'L0_ffn_w2': _L0_ffn_in['w2'], 'L0_ffn_b2': _L0_ffn_in['b2']}
    _x0 = _d['L0_attn_x']
    _d['L0_attn_x'] = jax.random.normal(jax.random.fold_in(jax.random.key(seed), 1), (8, 256, 128), dtype=_x0.dtype)
    del _x0
    return _d

def reference(L0_attn_x, L0_attn_w_norm, L0_attn_W_in, L0_attn_W_dt, L0_attn_b_dt, L0_attn_W_out, L0_ffn_w1, L0_ffn_b1, L0_ffn_w2, L0_ffn_b2):

    def _L0_attn_ref(x, w_norm, W_in, W_dt, b_dt, W_out):
        import jax, jax.numpy as jnp
        import numpy as np
        B, K, D = (8, 256, 128)
        INNER = 2 * D
        EPS = 1e-05

        def _silu(x):
            return x * jax.nn.sigmoid(x)
        h = x * jax.lax.rsqrt(jnp.mean(x * x, axis=-1, keepdims=True) + EPS) * w_norm
        uv = jnp.einsum('bkd,ed->bke', h, W_in)
        u, z = (uv[..., :INNER], uv[..., INNER:])
        u = _silu(u)
        lam = jax.nn.sigmoid(jnp.einsum('bki,ji->bkj', u, W_dt) + b_dt)

        def step(s, inp):
            lam_t, u_t = inp
            s = lam_t * s + (1.0 - lam_t) * u_t
            return (s, s)
        lam_k = jnp.moveaxis(lam, 1, 0)
        u_k = jnp.moveaxis(u, 1, 0)
        s0 = jnp.zeros((x.shape[0], INNER), dtype=x.dtype)
        _, ys = jax.lax.scan(step, s0, (lam_k, u_k))
        s = jnp.moveaxis(ys, 0, 1)
        s = s * _silu(z)
        y = jnp.einsum('bki,di->bkd', s, W_out)
        return x + y

    def _L0_ffn_ref(x, w1, b1, w2, b2):
        import jax, jax.numpy as jnp
        import numpy as np

        def _binarize(w):
            alpha = jax.lax.stop_gradient(jnp.mean(jnp.abs(w), axis=1, keepdims=True))
            bw = alpha * jnp.sign(w)
            return w + jax.lax.stop_gradient(bw - w)
        bw1 = _binarize(w1)
        h = jnp.einsum('bsd,hd->bsh', x, bw1) + b1
        h = jax.nn.gelu(h, approximate=False)
        bw2 = _binarize(w2)
        out = jnp.einsum('bsh,dh->bsd', h, bw2) + b2
        return out
    x = L0_attn_x
    x = _layernorm(x + _L0_attn_ref(x, L0_attn_w_norm, L0_attn_W_in, L0_attn_W_dt, L0_attn_b_dt, L0_attn_W_out), axis=-1)
    x = _layernorm(x + _L0_ffn_ref(x, L0_ffn_w1, L0_ffn_b1, L0_ffn_w2, L0_ffn_b2), axis=-1)
    return x

_drawn_inputs = setup_inputs


def setup_inputs(seed=0):
    import zlib

    import numpy as np

    out = dict(_drawn_inputs(seed))
    spreads = {'L0_attn_w_norm': (1.0, 0.2), 'L0_attn_b_dt': (0.0, 0.8)}
    factors = {'L0_ffn_b1': 8.0, 'L0_ffn_b2': 2.785}
    for name, (base, spread) in spreads.items():
        noise = np.random.default_rng([zlib.crc32(name.encode()), seed]).standard_normal(out[name].shape)
        drawn = base * np.exp(spread * noise) if base else spread * noise
        out[name] = jnp.asarray(drawn.astype(out[name].dtype))
    for name, factor in factors.items():
        out[name] = (out[name] * factor).astype(out[name].dtype)
    return out
```

```python
from contextlib import ExitStack

import concourse.bass as bass
from concourse import mybir

ALU = mybir.AluOpType
ACT = mybir.ActivationFunctionType
AX_X = mybir.AxisListType.X
F32 = mybir.dt.float32
F32R = mybir.dt.float32r

P = 128
RMS_EPS = 1e-5
LN_EPS = 1e-5


def gated_scan_then_binary_ffn(nc, x, w_norm, W_inT, W_dtT, b_dt, W_outT, w1, w1T, b1, w2, w2T, b2, out):
    TOK, D = x.shape
    INNER = W_dtT.shape[0]
    H = w1.shape[0]
    SEQ = 256
    GT = 512
    G = TOK // GT
    J = GT // P
    B = GT // SEQ
    C = INNER // P
    HC = H // P
    assert D == P and GT % SEQ == 0 and TOK % GT == 0

    half = G // 2
    chunks = []
    for first in (0, half):
        chunks += [(kind, g, c) for g in range(first, first + half) for kind in "uz" for c in range(C)]
        chunks += [("l", g, c) for g in range(first, first + half) for c in range(C)]
    chunks += [("h", g, c) for g in range(G) for c in range(HC)]
    nth = {key: i for i, key in enumerate(chunks)}
    BANKS = 5

    with ExitStack() as ctx:
        def sb(name, shape, dt=F32):
            return ctx.enter_context(nc.sbuf_tensor(name, shape, dt))

        def ps(name, shape):
            return ctx.enter_context(nc.psum_tensor(name, shape, F32))

        def sem(name):
            return ctx.enter_context(nc.semaphore(name))

        wnorm_sb = sb("wnorm_sb", [P, 1])
        win_sb = sb("win_sb", [P, 2 * INNER])
        wdt_sb = sb("wdt_sb", [P, C, INNER])
        wout_sb = sb("wout_sb", [P, C, D])
        bdt_sb = sb("bdt_sb", [P, C])
        w1_sb = sb("w1_sb", [P, HC, D])
        w1T_sb = sb("w1T_sb", [P, H])
        sign1 = sb("sign1", [P, H], F32R)
        alpha1 = sb("alpha1", [P, HC])
        b1_sb = sb("b1_sb", [P, HC])
        w2_sb = sb("w2_sb", [P, H])
        w2T_sb = sb("w2T_sb", [P, HC, D])
        sign2 = sb("sign2", [P, HC, D], F32R)
        alpha2 = sb("alpha2", [P, 1])
        b2_sb = sb("b2_sb", [P, 1])
        ident = sb("ident", [P, P])
        minus_half = sb("minus_half", [P, J])

        x_sb = sb("x_sb", [P, G, J, D])
        square = sb("square", [P, 2, D])
        sumsq = sb("sumsq", [P, G, J])
        meansq = sb("meansq", [P, G, J])
        rms_inv = sb("rms_inv", [P, G, J])
        xs = sb("xs", [P, 2, J, D])
        hT = sb("hT", [P, 2, GT])
        u = sb("u", [P, G, C, GT])
        z = sb("z", [P, G, C, GT])
        lam = sb("lam", [P, 2, C, GT])
        s = sb("s", [P, 2, C, GT])
        yT = sb("yT", [P, 2, J, P])
        v1 = sb("v1", [P, 2, J, D])
        stats = sb("stats", [P, 2, J, 6])
        mv1 = sb("mv1", [P, G, J, 2])
        vare1 = sb("vare1", [P, G, J])
        rstd1 = sb("rstd1", [P, G, J])
        x1 = sb("x1", [P, G, J, D])
        x1T_hi = sb("x1T_hi", [P, 2, GT], F32R)
        x1T_lo = sb("x1T_lo", [P, 2, GT], F32R)
        hid = sb("hid", [P, 2, HC, GT])
        hid_hi = sb("hid_hi", [P, 2, HC, GT], F32R)
        hid_lo = sb("hid_lo", [P, 2, HC, GT], F32R)
        oT = sb("oT", [P, 2, J, P])
        v2 = sb("v2", [P, 2, J, D])
        mv2 = sb("mv2", [P, G, J, 2])
        vare2 = sb("vare2", [P, G, J])
        rstd2 = sb("rstd2", [P, G, J])
        y = sb("y", [P, G, J, D])

        turn = ps("turn", [P, GT])
        acc = ps("acc", [P, GT])
        back = ps("back", [P, GT])
        wide = [ps(f"wide{i}", [P, GT]) for i in range(BANKS)]

        x_in = [sem(f"x_in{g}") for g in range(G)]
        wnorm_in, win_in, wdt_in, wout_in, bdt_in = (
            sem(n) for n in ("wnorm_in", "win_in", "wdt_in", "wout_in", "bdt_in"))
        w1_in, w1T_in, b1_in, w2_in, w2T_in, b2_in = (
            sem(n) for n in ("w1_in", "w1T_in", "b1_in", "w2_in", "w2T_in", "b2_in"))
        zeroed = sem("zeroed")
        ident_ready = sem("ident_ready")
        power_ready = sem("power_ready")
        sumsq_ready = sem("sumsq_ready")
        meansq_ready = sem("meansq_ready")
        rms_ready = sem("rms_ready")
        xs_ready = sem("xs_ready")
        xT_ready = sem("xT_ready")
        hT_ready = sem("hT_ready")
        chunk_ready = sem("chunk_ready")
        chunk_taken = sem("chunk_taken")
        drive_ready = sem("drive_ready")
        scan_done = sem("scan_done")
        gated_ready = sem("gated_ready")
        acc_ready = sem("acc_ready")
        acc_taken = sem("acc_taken")
        back_ready = sem("back_ready")
        back_taken = sem("back_taken")
        stats_done = sem("stats_done")
        var1_ready = sem("var1_ready")
        vare_ready = sem("vare_ready")
        rstd1_ready = sem("rstd1_ready")
        x1_ready = sem("x1_ready")
        x1T_ready = sem("x1T_ready")
        x1hi_ready = sem("x1hi_ready")
        x1lo_ready = sem("x1lo_ready")
        signs_ready = sem("signs_ready")
        abs_sums = sem("abs_sums")
        alphas_ready = sem("alphas_ready")
        hidlo_ready = sem("hidlo_ready")
        var2_ready = sem("var2_ready")
        rstd2_ready = sem("rstd2_ready")
        y_ready = sem("y_ready")
        stored = sem("stored")

        block = ctx.enter_context(nc.Block())

        x_dram = x.rearrange("(g p j) d -> g p j d", p=P, j=J)
        out_dram = out.rearrange("(g p j) d -> g p j d", p=P, j=J)

        @block.sync
        def _(sp):
            sp.dma_start(x_sb[:, 0], x_dram[0]).then_inc(x_in[0], 16)
            sp.dma_start(win_sb[:], W_inT).then_inc(win_in, 16)
            for g in range(1, G):
                sp.dma_start(x_sb[:, g], x_dram[g]).then_inc(x_in[g], 16)
            sp.dma_start(wdt_sb[:], W_dtT.rearrange("(c p) n -> p c n", p=P)).then_inc(wdt_in, 16)
            sp.dma_start(wout_sb[:], W_outT.rearrange("(c p) n -> p c n", p=P)).then_inc(wout_in, 16)
            for g in range(G):
                sp.wait_ge(y_ready, g + 1)
                sp.dma_start(out_dram[g], y[:, g]).then_inc(stored, 16)
            sp.wait_ge(stored, 16 * G)

        @block.gpsimd
        def _(pool):
            nc.gpsimd.memset(ident[:], 0.0).then_inc(zeroed, 1)
            nc.gpsimd.memset(minus_half[:], -0.5).then_inc(power_ready, 1)
            pool.wait_ge(zeroed, 1)
            nc.gpsimd.affine_select(out=ident[:], in_=ident[:], compare_op=ALU.not_equal, fill=1.0, base=0,
                                    pattern=[[-1, P]], channel_multiplier=1).then_inc(ident_ready, 1)
            pool.wait_ge(power_ready, 1)

            def inverse_root(dst, mid, src, mul, eps, n, ready):
                nc.gpsimd.tensor_scalar(mid, src, mul, eps, ALU.mult, ALU.add).then_inc(vare_ready, 1)
                pool.wait_ge(vare_ready, n)
                nc.gpsimd.tensor_tensor(dst, mid, minus_half[:], ALU.pow).then_inc(ready, 1)

            for g in range(G):
                pool.wait_ge(sumsq_ready, J * (g + 1))
                inverse_root(rms_inv[:, g], meansq[:, g], sumsq[:, g], 1.0 / D, RMS_EPS, g + 1, rms_ready)
            for g in range(G):
                pool.wait_ge(var1_ready, J * (g + 1))
                inverse_root(rstd1[:, g], vare1[:, g], mv1[:, g, :, 1], 1.0, LN_EPS, G + g + 1, rstd1_ready)
            for g in range(G):
                pool.wait_ge(var2_ready, J * (g + 1))
                inverse_root(rstd2[:, g], vare2[:, g], mv2[:, g, :, 1], 1.0, LN_EPS, 2 * G + g + 1, rstd2_ready)

        @block.scalar
        def _(act):
            act.dma_start(wnorm_sb[:], w_norm).then_inc(wnorm_in, 16)
            act.dma_start(bdt_sb[:], b_dt).then_inc(bdt_in, 16)
            act.dma_start(w1T_sb[:], w1T).then_inc(w1T_in, 16)
            act.dma_start(w2T_sb[:], w2T.rearrange("(c p) d -> p c d", p=P)).then_inc(w2T_in, 16)
            act.dma_start(w1_sb[:], w1.rearrange("(c p) d -> p c d", p=P)).then_inc(w1_in, 16)
            act.dma_start(w2_sb[:], w2).then_inc(w2_in, 16)
            act.dma_start(b1_sb[:], b1).then_inc(b1_in, 16)
            act.dma_start(b2_sb[:], b2).then_inc(b2_in, 16)

            def norm_weight(g):
                act.wait_ge(xT_ready, g + 1)
                if g >= 2:
                    act.wait_ge(chunk_ready, nth["z", g - 2, C - 1] + 1)
                nc.scalar.activation(hT[:, g % 2, :].rearrange("d (p j) -> d j p", j=J),
                                     turn[:].rearrange("d (j p) -> d j p", j=J),
                                     ACT.Copy, scale=wnorm_sb[:, 0:1]).then_inc(hT_ready, 1)

            def take(key, dst, func, **more):
                i = nth[key]
                act.wait_ge(chunk_ready, i + 1)
                return nc.scalar.activation(dst, wide[i % BANKS][:], func, **more)

            def silus(g):
                for kind, dst in (("u", u), ("z", z)):
                    for c in range(C):
                        take((kind, g, c), dst[:, g, c], ACT.Silu).then_inc(chunk_taken, 1)

            def gates(g):
                if g >= 2:
                    act.wait_ge(scan_done, B * C * (g - 1))
                for c in range(C):
                    take(("l", g, c), lam[:, g % 2, c], ACT.Sigmoid, bias=bdt_sb[:, c:c + 1]).then_inc(chunk_taken, 1)

            def scan_out(g):
                act.wait_ge(acc_ready, g + 1)
                nc.scalar.activation(yT[:, g % 2], acc[:].rearrange("d (p j) -> d j p", j=J),
                                     ACT.Copy).then_inc(acc_taken, 1)

            def x1_hi(g):
                act.wait_ge(x1T_ready, g + 1)
                if g >= 2:
                    act.wait_ge(chunk_ready, nth["h", g - 2, HC - 1] + 1)
                nc.scalar.activation(x1T_hi[:, g % 2], turn[:], ACT.Copy).then_inc(x1hi_ready, 1)

            def gelus(g):
                if g >= 2:
                    act.wait_ge(acc_ready, G + g - 1)
                    act.wait_ge(hidlo_ready, HC * (g - 1))
                for c in range(HC):
                    more = dict(scale=alpha1[:, c:c + 1], bias=b1_sb[:, c:c + 1])
                    take(("h", g, c), hid[:, g % 2, c], ACT.Gelu, **more)
                    take(("h", g, c), hid_hi[:, g % 2, c], ACT.Gelu, **more).then_inc(chunk_taken, 1)

            def ffn_out(g):
                act.wait_ge(acc_ready, G + g + 1)
                nc.scalar.activation(oT[:, g % 2], acc[:].rearrange("d (j p) -> d j p", j=J), ACT.Identity,
                                     scale=alpha2[:, 0:1], bias=b2_sb[:, 0:1]).then_inc(acc_taken, 1)

            act.wait_ge(wnorm_in, 16)
            norm_weight(0)
            norm_weight(1)
            silus(0)
            silus(1)
            act.wait_ge(w1T_in, 16)
            nc.scalar.activation(sign1[:], w1T_sb[:], ACT.Sign).then_inc(signs_ready, 1)
            act.wait_ge(w2T_in, 16)
            nc.scalar.activation(sign2[:], w2T_sb[:], ACT.Sign).then_inc(signs_ready, 1)
            act.wait_ge(bdt_in, 16)
            gates(0)
            norm_weight(2)
            gates(1)
            norm_weight(3)
            scan_out(0)
            silus(2)
            scan_out(1)
            silus(3)
            gates(2)
            x1_hi(0)
            gates(3)
            scan_out(2)
            x1_hi(1)
            act.wait_ge(b1_in, 16)
            act.wait_ge(b2_in, 16)
            act.wait_ge(alphas_ready, 2)
            gelus(0)
            scan_out(3)
            gelus(1)
            ffn_out(0)
            x1_hi(2)
            gelus(2)
            ffn_out(1)
            x1_hi(3)
            gelus(3)
            ffn_out(2)
            ffn_out(3)

        @block.tensor
        def _(pe):
            def turn_x(g):
                pe.wait_ge(xs_ready, g + 1)
                if g >= 1:
                    pe.wait_ge(hT_ready, g)
                for j in range(J):
                    last = nc.tensor.transpose(turn[:, j * P:(j + 1) * P], xs[:, g % 2, j], ident[:])
                last.then_inc(xT_ready, 1)

            def bank(key):
                i = nth[key]
                if i >= BANKS:
                    pe.wait_ge(chunk_taken, i - BANKS + 1)
                return wide[i % BANKS][:]

            def project_in(g):
                pe.wait_ge(hT_ready, g + 1)
                for k, kind in enumerate("uz"):
                    for c in range(C):
                        e = k * INNER + c * P
                        nc.tensor.matmul(bank((kind, g, c)), win_sb[:, e:e + P], hT[:, g % 2],
                                         start=True, stop=True).then_inc(chunk_ready, 1)

            def project_gate(g):
                pe.wait_ge(chunk_taken, nth["u", g, C - 1] + 1)
                for c in range(C):
                    dst = bank(("l", g, c))
                    for k in range(C):
                        last = nc.tensor.matmul(dst, wdt_sb[:, k, c * P:(c + 1) * P], u[:, g, k],
                                                start=(k == 0), stop=(k == C - 1))
                    last.then_inc(chunk_ready, 1)

            def project_out(g):
                pe.wait_ge(gated_ready, g + 1)
                if g >= 1:
                    pe.wait_ge(acc_taken, g)
                for k in range(C):
                    last = nc.tensor.matmul(acc[:], wout_sb[:, k], z[:, g, k], start=(k == 0), stop=(k == C - 1))
                last.then_inc(acc_ready, 1)

            def turn_back(n, src):
                pe.wait_ge(acc_taken, n + 1)
                if n >= 1:
                    pe.wait_ge(back_taken, n)
                for j in range(J):
                    last = nc.tensor.transpose(back[:, j * P:(j + 1) * P], src[:, n % 2, j], ident[:])
                last.then_inc(back_ready, 1)

            def turn_x1(g):
                pe.wait_ge(x1_ready, J * (g + 1))
                if g >= 1:
                    pe.wait_ge(x1hi_ready, g)
                    pe.wait_ge(x1lo_ready, g)
                for j in range(J):
                    last = nc.tensor.transpose(turn[:, j * P:(j + 1) * P], x1[:, g, j], ident[:])
                last.then_inc(x1T_ready, 1)

            def ffn_in(g):
                pe.wait_ge(x1hi_ready, g + 1)
                pe.wait_ge(x1lo_ready, g + 1)
                for c in range(HC):
                    dst = bank(("h", g, c))
                    w = sign1[:, c * P:(c + 1) * P]
                    nc.tensor.matmul(dst, w, x1T_lo[:, g % 2], start=True, stop=False)
                    nc.tensor.matmul(dst, w, x1T_hi[:, g % 2], start=False, stop=True).then_inc(chunk_ready, 1)

            def ffn_back(g):
                pe.wait_ge(acc_taken, G + g)
                for c in range(HC):
                    pe.wait_ge(hidlo_ready, HC * g + c + 1)
                    nc.tensor.matmul(acc[:], sign2[:, c], hid_lo[:, g % 2, c], start=(c == 0), stop=False)
                    last = nc.tensor.matmul(acc[:], sign2[:, c], hid_hi[:, g % 2, c], start=False, stop=(c == HC - 1))
                last.then_inc(acc_ready, 1)

            pe.wait_ge(ident_ready, 1)
            turn_x(0)
            turn_x(1)
            pe.wait_ge(win_in, 16)
            project_in(0)
            turn_x(2)
            project_in(1)
            pe.wait_ge(wdt_in, 16)
            project_gate(0)
            project_gate(1)
            turn_x(3)
            pe.wait_ge(wout_in, 16)
            project_in(2)
            project_out(0)
            turn_back(0, yT)
            project_in(3)
            project_out(1)
            turn_back(1, yT)
            project_gate(2)
            turn_x1(0)
            project_gate(3)
            project_out(2)
            turn_back(2, yT)
            pe.wait_ge(signs_ready, 2)
            turn_x1(1)
            ffn_in(0)
            project_out(3)
            turn_back(3, yT)
            ffn_in(1)
            ffn_back(0)
            turn_x1(2)
            turn_back(G + 0, oT)
            ffn_in(2)
            ffn_back(1)
            turn_x1(3)
            turn_back(G + 1, oT)
            ffn_in(3)
            ffn_back(2)
            turn_back(G + 2, oT)
            ffn_back(3)
            turn_back(G + 3, oT)

        @block.vector
        def _(dve):
            def sums_of_squares(g):
                dve.wait_ge(x_in[g], 16)
                for j in range(J):
                    if g or j >= 2:
                        dve.wait_ge(sumsq_ready, J * g + j - 1)
                    nc.vector.tensor_tensor_reduce(square[:, j % 2], x_sb[:, g, j], x_sb[:, g, j], 1.0, 0.0,
                                                   ALU.mult, ALU.add, sumsq[:, g, j:j + 1]).then_inc(sumsq_ready, 1)

            def scale_rows(g):
                dve.wait_ge(rms_ready, g + 1)
                if g >= 2:
                    dve.wait_ge(xT_ready, g - 1)
                nc.vector.tensor_tensor(xs[:, g % 2], x_sb[:, g], rms_inv[:, g, :, None].to_broadcast([P, J, D]),
                                        ALU.mult).then_inc(xs_ready, 1)

            def drive(g):
                dve.wait_ge(chunk_taken, nth["l", g, C - 1] + 1)
                if g >= 2:
                    dve.wait_ge(gated_ready, g - 1)
                nc.vector.scalar_tensor_tensor(out=s[:, g % 2], in0=lam[:, g % 2], scalar=1.0, in1=u[:, g],
                                               op0=ALU.subtract, op1=ALU.mult).then_inc(drive_ready, 1)

            def scan(g):
                dve.wait_ge(drive_ready, g + 1)
                for c in range(C):
                    for b in range(B):
                        at = slice(b * SEQ, (b + 1) * SEQ)
                        nc.vector.tensor_tensor_scan(s[:, g % 2, c, at], lam[:, g % 2, c, at], s[:, g % 2, c, at],
                                                     0.0, ALU.mult, ALU.subtract).then_inc(scan_done, 1)

            def gate_out(g):
                dve.wait_ge(scan_done, B * C * (g + 1))
                nc.vector.tensor_tensor(z[:, g], s[:, g % 2], z[:, g], ALU.mult).then_inc(gated_ready, 1)

            def statistics(v, mv, n, ready):
                dve.wait_ge(back_taken, n + 1)
                for j in range(J):
                    nc.vector.bn_stats(stats[:, n % 2, j], v[:, n % 2, j]).then_inc(stats_done, 1)
                for j in range(J):
                    dve.wait_ge(stats_done, J * n + j + 1)
                    nc.vector.bn_aggr(mv[:, n % G, j], stats[:, n % 2, j]).then_inc(ready, 1)

            def residual1(g):
                dve.wait_ge(back_ready, g + 1)
                nc.vector.scalar_tensor_tensor(out=v1[:, g % 2], in0=x_sb[:, g], scalar=2.0,
                                               in1=back[:].rearrange("p (j d) -> p j d", j=J),
                                               op0=ALU.mult, op1=ALU.add).then_inc(back_taken, 1)
                statistics(v1, mv1, g, var1_ready)

            def normalise(dst, v, mv, rstd, g, done):
                for j in range(J):
                    nc.vector.tensor_scalar(dst[:, g, j], v[:, g % 2, j], mv[:, g, j, 0:1], rstd[:, g, j:j + 1],
                                            ALU.subtract, ALU.mult).then_inc(done, 1)

            def layernorm1(g):
                dve.wait_ge(rstd1_ready, g + 1)
                normalise(x1, v1, mv1, rstd1, g, x1_ready)

            def x1_lo(g):
                dve.wait_ge(x1hi_ready, g + 1)
                if g >= 2:
                    dve.wait_ge(chunk_ready, nth["h", g - 2, HC - 1] + 1)
                nc.vector.tensor_tensor(x1T_lo[:, g % 2], turn[:], x1T_hi[:, g % 2].bitcast(F32),
                                        ALU.subtract).then_inc(x1lo_ready, 1)

            def hid_low(g):
                if g >= 2:
                    dve.wait_ge(acc_ready, G + g - 1)
                for c in range(HC):
                    dve.wait_ge(chunk_taken, nth["h", g, c] + 1)
                    nc.vector.tensor_tensor(hid_lo[:, g % 2, c], hid[:, g % 2, c], hid_hi[:, g % 2, c].bitcast(F32),
                                            ALU.subtract).then_inc(hidlo_ready, 1)

            def residual2(g):
                dve.wait_ge(back_ready, G + g + 1)
                nc.vector.tensor_tensor(v2[:, g % 2], x1[:, g], back[:].rearrange("p (j d) -> p j d", j=J),
                                        ALU.add).then_inc(back_taken, 1)
                statistics(v2, mv2, G + g, var2_ready)

            def layernorm2(g):
                dve.wait_ge(rstd2_ready, g + 1)
                for j in range(J):
                    last = nc.vector.tensor_scalar(y[:, g, j], v2[:, g % 2, j], mv2[:, g, j, 0:1], rstd2[:, g, j:j + 1],
                                                   ALU.subtract, ALU.mult)
                last.then_inc(y_ready, 1)

            def row_scales():
                dve.wait_ge(w1_in, 16)
                nc.vector.tensor_reduce(alpha1[:], w1_sb[:], AX_X, ALU.add,
                                        apply_absolute_value=True).then_inc(abs_sums, 1)
                dve.wait_ge(w2_in, 16)
                nc.vector.tensor_reduce(alpha2[:], w2_sb[:], AX_X, ALU.add,
                                        apply_absolute_value=True).then_inc(abs_sums, 1)
                dve.wait_ge(abs_sums, 2)
                nc.vector.tensor_scalar(alpha1[:], alpha1[:], 1.0 / D, None, ALU.mult).then_inc(alphas_ready, 1)
                nc.vector.tensor_scalar(alpha2[:], alpha2[:], 1.0 / H, None, ALU.mult).then_inc(alphas_ready, 1)

            sums_of_squares(0)
            sums_of_squares(1)
            scale_rows(0)
            sums_of_squares(2)
            scale_rows(1)
            sums_of_squares(3)
            scale_rows(2)
            scale_rows(3)
            row_scales()
            drive(0)
            scan(0)
            gate_out(0)
            drive(1)
            scan(1)
            gate_out(1)
            residual1(0)
            layernorm1(0)
            residual1(1)
            x1_lo(0)
            layernorm1(1)
            drive(2)
            scan(2)
            gate_out(2)
            x1_lo(1)
            drive(3)
            scan(3)
            gate_out(3)
            residual1(2)
            hid_low(0)
            layernorm1(2)
            residual1(3)
            x1_lo(2)
            hid_low(1)
            layernorm1(3)
            residual2(0)
            x1_lo(3)
            hid_low(2)
            layernorm2(0)
            residual2(1)
            hid_low(3)
            layernorm2(1)
            residual2(2)
            layernorm2(2)
            residual2(3)
            layernorm2(3)


def kernel(L0_attn_x, L0_attn_w_norm, L0_attn_W_in, L0_attn_W_dt, L0_attn_b_dt, L0_attn_W_out,
           L0_ffn_w1, L0_ffn_b1, L0_ffn_w2, L0_ffn_b2):
    import numpy as _np
    import concourse.bacc as _bacc
    from concourse import mybir as _mybir
    from concourse.bass_utils import run_bass_kernel_spmd as _run

    def columns(v):
        return _np.asarray(v).reshape(-1, P).T

    shape = _np.asarray(L0_attn_x).shape
    laid_out = {
        "x": _np.asarray(L0_attn_x).reshape(-1, shape[-1]),
        "w_norm": columns(L0_attn_w_norm),
        "W_inT": _np.asarray(L0_attn_W_in).T,
        "W_dtT": _np.asarray(L0_attn_W_dt).T,
        "b_dt": columns(L0_attn_b_dt),
        "W_outT": _np.asarray(L0_attn_W_out).T,
        "w1": _np.asarray(L0_ffn_w1),
        "w1T": _np.asarray(L0_ffn_w1).T,
        "b1": columns(L0_ffn_b1),
        "w2": _np.asarray(L0_ffn_w2),
        "w2T": _np.asarray(L0_ffn_w2).T,
        "b2": columns(L0_ffn_b2),
    }
    nc = _bacc.Bacc("TRN2", target_bir_lowering=False, num_devices=1)
    arrays, args = {}, []
    for name, a in laid_out.items():
        a = _np.ascontiguousarray(a)
        arrays[f"in_{name}"] = a
        args.append(nc.dram_tensor(f"in_{name}", a.shape, _mybir.dt.from_np(a.dtype), kind="ExternalInput").ap())
    args.append(nc.dram_tensor("out_y", laid_out["x"].shape, _mybir.dt.float32, kind="ExternalOutput").ap())
    gated_scan_then_binary_ffn(nc, *args)
    r = _run(nc, [arrays], core_ids=[0])
    return r.results[0]["out_y"].reshape(shape)
```

```python
from contextlib import ExitStack

import concourse.bass as bass
from concourse import mybir

ALU = mybir.AluOpType
ACT = mybir.ActivationFunctionType
AX_X = mybir.AxisListType.X
F32 = mybir.dt.float32
F32R = mybir.dt.float32r

P = 128
RMS_EPS = 1e-5
LN_EPS = 1e-5


def gated_scan_then_binary_ffn(nc, x, w_norm, W_inT, W_dtT, b_dt, W_outT, w1, w1T, b1, w2, w2T, b2, out):
    TOK, D = x.shape
    INNER = W_dtT.shape[0]
    H = w1T.shape[1]
    SEQ = 256
    GT = 512
    G = TOK // GT
    J = GT // P
    B = GT // SEQ
    C = INNER // P
    HC = H // P
    assert D == P and GT % SEQ == 0 and TOK % GT == 0

    steps = [("u", 0, 0), ("u", 0, 1), ("z", 0, 0), ("z", 0, 1), ("l", 0, 0), ("l", 0, 1), ("u", 1, 0), ("u", 1,
             1), ("z", 1, 0), ("z", 1, 1), ("l", 1, 0), ("l", 1, 1), ("u", 2, 0), ("u", 2, 1), ("z", 2, 0), ("l",
             2, 0), ("l", 2, 1), ("u", 3, 0), ("z", 2, 1), ("u", 3, 1), ("z", 3, 0), ("z", 3, 1), ("l", 3, 0),
             ("l", 3, 1), ("h", 0, 0), ("h", 0, 1), ("h", 0, 2), ("h", 0, 3), ("h", 1, 0), ("h", 1, 1), ("h", 1,
             2), ("h", 1, 3), ("h", 2, 0), ("h", 2, 1), ("h", 2, 2), ("h", 2, 3), ("h", 3, 0), ("h", 3, 1), ("h",
             3, 2), ("h", 3, 3)]
    nth = {step: i for i, step in enumerate(steps)}
    assert len(nth) == G * (3 * C + HC)
    BANKS = 4

    PIECES = [[(0, 2), (2, 4)]] * (G - 1) + [[(0, 2), (2, 3), (3, 4)]]
    pieces_before = [sum(len(p) for p in PIECES[:g]) for g in range(G)]

    rows_order = [("a", 0, 0), ("s", 0, 0), ("s", 1, 0), ("s", 2, 0), ("y", 0, 0), ("s", 3, 0), ("y", 0, 1), ("y", 1,
                  0), ("y", 1, 1), ("y", 2, 0), ("y", 2, 1), ("y", 3, 0), ("y", 3, 1), ("y", 3, 2)]
    assert len(rows_order) == G + 1 + sum(len(p) for p in PIECES)
    ROW_BANKS = 3
    by_scalar = {(0, 1), (1, 0), (2, 1)}
    WARM = 18

    def unit(kind, g, piece=0):
        return rows_order.index((kind, g, piece))

    def read_last(kinds, g):
        return max(i for (kind, of, c), i in nth.items() if kind in kinds and of == g) + 1

    with ExitStack() as ctx:
        def sb(name, shape, dt=F32):
            return ctx.enter_context(nc.sbuf_tensor(name, shape, dt))

        def ps(name, shape):
            return ctx.enter_context(nc.psum_tensor(name, shape, F32))

        def sem(name):
            return ctx.enter_context(nc.semaphore(name))

        wnorm_sb = sb("wnorm_sb", [P, 1])
        win_sb = sb("win_sb", [P, 2 * INNER])
        win_hi = sb("win_hi", [P, 2 * INNER], F32R)
        win_lo = sb("win_lo", [P, 2 * INNER], F32R)
        wdt_sb = sb("wdt_sb", [P, C, INNER])
        wout_sb = sb("wout_sb", [P, C, D])
        bdt_sb = sb("bdt_sb", [P, C])
        w1T_sb = sb("w1T_sb", [P, H])
        sign1 = sb("sign1", [P, H], F32R)
        w1_sb = sb("w1_sb", [P, HC, D])
        sum1 = sb("sum1", [P, HC])
        alpha1 = sb("alpha1", [P, HC])
        b1_sb = sb("b1_sb", [P, HC])
        w2T_sb = sb("w2T_sb", [P, HC, D])
        sign2 = sb("sign2", [P, HC, D])
        w2_sb = sb("w2_sb", [P, H])
        sum2 = sb("sum2", [P, 1])
        diag2 = sb("diag2", [P, D])
        bw2T = sb("bw2T", [P, HC, D])
        b2_sb = sb("b2_sb", [P, D])
        ident = sb("ident", [P, P])
        ones = sb("ones", [P, P])
        minus_half = sb("minus_half", [P, J])

        x_sb = sb("x_sb", [P, G, J, D])
        square = sb("square", [P, 2, D])
        meansq = sb("meansq", [P, G, J])
        rms_inv = sb("rms_inv", [P, G, J])
        xs = sb("xs", [P, 2, J, D])
        hT_hi = sb("hT_hi", [P, 2, GT], F32R)
        hT_lo = sb("hT_lo", [P, 2, GT], F32R)
        u = sb("u", [P, G, C, GT])
        z = sb("z", [P, G, C, GT])
        lam = sb("lam", [P, 2, C, GT])
        s = sb("s", [P, 2, C, GT])
        gated = sb("gated", [P, 2, C, J, P])
        v1 = sb("v1", [P, G, J, D])
        stats1 = sb("stats1", [P, G, J, 6])
        stats2 = sb("stats2", [P, G, J, 6])
        mv1 = sb("mv1", [P, G, J, 2])
        vare1 = sb("vare1", [P, G, J])
        rstd1 = sb("rstd1", [P, G, J])
        x1 = sb("x1", [P, G, J, D])
        x1b = sb("x1b", [P, G, J, D])
        x1T_hi = sb("x1T_hi", [P, 2, GT], F32R)
        x1T_lo = sb("x1T_lo", [P, 2, GT], F32R)
        hid = sb("hid", [P, 2, HC, GT])
        v2 = sb("v2", [P, G, J, D])
        mv2 = sb("mv2", [P, G, J, 2])
        vare2 = sb("vare2", [P, G, J])
        rstd2 = sb("rstd2", [P, G, J])
        minus_m2 = sb("minus_m2", [P, G, J])
        shift2 = sb("shift2", [P, G, J])
        y = sb("y", [P, G, J, D])

        turn = ps("turn", [P, GT])
        rows = [ps(f"rows{i}", [P, J, D]) for i in range(ROW_BANKS)]
        wide = [ps(f"wide{i}", [P, GT]) for i in range(BANKS)]

        x_in = [sem(f"x_in{g}") for g in range(G)]
        wnorm_in, win_in, wdt_in, wout_in, bdt_in = (
            sem(n) for n in ("wnorm_in", "win_in", "wdt_in", "wout_in", "bdt_in"))
        w1_in, w1T_in, b1_in, w2_in, w2T_in, b2_in = (
            sem(n) for n in ("w1_in", "w1T_in", "b1_in", "w2_in", "w2T_in", "b2_in"))
        zeroed = sem("zeroed")
        ident_ready = sem("ident_ready")
        power_ready = sem("power_ready")
        ones_ready = sem("ones_ready")
        winhi_ready = sem("winhi_ready")
        winlo_ready = sem("winlo_ready")
        meansq_ready = sem("meansq_ready")
        rms_ready = sem("rms_ready")
        xs_ready = sem("xs_ready")
        xT_ready = sem("xT_ready")
        hThi_ready = sem("hThi_ready")
        hTlo_ready = sem("hTlo_ready")
        chunk_ready = sem("chunk_ready")
        chunk_taken = sem("chunk_taken")
        drive_ready = sem("drive_ready")
        scan_done = sem("scan_done")
        gated_ready = sem("gated_ready")
        rows_ready = sem("rows_ready")
        rows_taken = sem("rows_taken")
        stats1_done = sem("stats1_done")
        stats2_done = sem("stats2_done")
        var1_ready = sem("var1_ready")
        vare_ready = sem("vare_ready")
        rstd1_ready = sem("rstd1_ready")
        x1_ready = sem("x1_ready")
        x1b_ready = sem("x1b_ready")
        x1T_ready = sem("x1T_ready")
        x1hi_ready = sem("x1hi_ready")
        x1lo_ready = sem("x1lo_ready")
        sign1_ready = sem("sign1_ready")
        sign2_ready = sem("sign2_ready")
        sum1_ready = sem("sum1_ready")
        sum2_ready = sem("sum2_ready")
        diag2_ready = sem("diag2_ready")
        alpha1_ready = sem("alpha1_ready")
        var2_ready = sem("var2_ready")
        rstd2_ready = sem("rstd2_ready")
        minus_m2_ready = sem("minus_m2_ready")
        shift2_ready = sem("shift2_ready")
        y_ready = [[sem(f"y_ready{g}_{i}") for i in range(len(PIECES[g]))] for g in range(G)]
        stored = sem("stored")

        block = ctx.enter_context(nc.Block())

        x_dram = x.rearrange("(g p j) d -> g p j d", p=P, j=J)
        out_dram = out.rearrange("(g p j) d -> g p j d", p=P, j=J)

        @block.sync
        def _(sp):
            def load_x(g):
                sp.dma_start(x_sb[:, g], x_dram[g]).then_inc(x_in[g], 16)

            load_x(0)
            sp.dma_start(win_sb[:], W_inT).then_inc(win_in, 16)
            sp.dma_start(wnorm_sb[:], w_norm).then_inc(wnorm_in, 16)
            load_x(1)
            load_x(2)
            sp.dma_start(wdt_sb[:], W_dtT.rearrange("(c p) n -> p c n", p=P)).then_inc(wdt_in, 16)
            load_x(3)
            sp.dma_start(bdt_sb[:], b_dt).then_inc(bdt_in, 16)
            sp.dma_start(wout_sb[:], W_outT.rearrange("(c p) n -> p c n", p=P)).then_inc(wout_in, 16)
            sp.dma_start(w2T_sb[:], w2T.rearrange("(c p) d -> p c d", p=P)).then_inc(w2T_in, 16)
            sp.dma_start(w1T_sb[:], w1T).then_inc(w1T_in, 16)
            sp.dma_start(w1_sb[:], w1.rearrange("(c p) d -> p c d", p=P)).then_inc(w1_in, 16)
            sp.dma_start(w2_sb[:], w2).then_inc(w2_in, 16)
            sp.dma_start(b1_sb[:], b1).then_inc(b1_in, 16)
            sp.dma_start(b2_sb[:], b2.to_broadcast([P, D])).then_inc(b2_in, 16)
            for g in range(G):
                for i, (a, b) in enumerate(PIECES[g]):
                    sp.wait_ge(y_ready[g][i], 1)
                    sp.dma_start(out_dram[g][:, a:b], y[:, g, a:b]).then_inc(stored, 16)
            sp.wait_ge(stored, 16 * len(PIECES[G - 1]) + 16 * pieces_before[G - 1])

        @block.gpsimd
        def _(pool):
            nc.gpsimd.memset(ident[:], 0.0).then_inc(zeroed, 1)
            nc.gpsimd.memset(minus_half[:], -0.5).then_inc(power_ready, 1)
            pool.wait_ge(zeroed, 1)
            nc.gpsimd.affine_select(out=ident[:], in_=ident[:], compare_op=ALU.not_equal, fill=1.0, base=0,
                                    pattern=[[-1, P]], channel_multiplier=1).then_inc(ident_ready, 1)
            nc.gpsimd.memset(ones[:], 1.0).then_inc(ones_ready, 1)
            pool.wait_ge(power_ready, 1)

            def inverse_rms(g, a, b):
                pool.wait_ge(meansq_ready, J * g + b)
                nc.gpsimd.tensor_tensor(rms_inv[:, g, a:b], meansq[:, g, a:b], minus_half[:, a:b],
                                        ALU.pow).then_inc(rms_ready, b - a)

            def inverse_root(dst, mid, var, ready):
                nonlocal roots
                nc.gpsimd.tensor_scalar(mid, var, LN_EPS, None, ALU.add).then_inc(vare_ready, 1)
                roots += 1
                pool.wait_ge(vare_ready, roots)
                nc.gpsimd.tensor_tensor(dst, mid, minus_half[:, 0:dst.shape[1]], ALU.pow).then_inc(ready, 1)

            roots = 0

            def inverse_deviation1(g):
                pool.wait_ge(var1_ready, J * (g + 1))
                inverse_root(rstd1[:, g], vare1[:, g], mv1[:, g, :, 1], rstd1_ready)

            def inverse_deviation2(g, i):
                nonlocal shifts
                a, b = PIECES[g][i]
                pool.wait_ge(var2_ready, J * g + b)
                if (g, i) in by_scalar:
                    nc.gpsimd.tensor_scalar(minus_m2[:, g, a:b], mv2[:, g, a:b, 0], -1.0, None,
                                            ALU.mult).then_inc(minus_m2_ready, 1)
                inverse_root(rstd2[:, g, a:b], vare2[:, g, a:b], mv2[:, g, a:b, 1], rstd2_ready)
                if (g, i) in by_scalar:
                    shifts += 1
                    pool.wait_ge(minus_m2_ready, shifts)
                    pool.wait_ge(rstd2_ready, pieces_before[g] + i + 1)
                    nc.gpsimd.tensor_tensor(shift2[:, g, a:b], minus_m2[:, g, a:b], rstd2[:, g, a:b],
                                            ALU.mult).then_inc(shift2_ready, 1)

            shifts = 0

            inverse_rms(0, 0, 2)
            inverse_rms(0, 2, 4)
            inverse_rms(1, 0, J)
            inverse_rms(2, 0, J)
            inverse_rms(3, 0, J)
            inverse_deviation1(0)
            inverse_deviation1(1)
            inverse_deviation1(2)
            inverse_deviation2(0, 0)
            inverse_deviation1(3)
            inverse_deviation2(0, 1)
            inverse_deviation2(1, 0)
            inverse_deviation2(1, 1)
            inverse_deviation2(2, 0)
            inverse_deviation2(2, 1)
            inverse_deviation2(3, 0)
            inverse_deviation2(3, 1)
            inverse_deviation2(3, 2)

        @block.scalar
        def _(act):
            def norm_weight(g):
                act.wait_ge(xT_ready, g + 1)
                if g >= 2:
                    act.wait_ge(chunk_ready, read_last("uz", g - 2))
                nc.scalar.activation(hT_hi[:, g % 2, :].rearrange("d (p j) -> d j p", j=J),
                                     turn[:].rearrange("d (j p) -> d j p", j=J),
                                     ACT.Copy, scale=wnorm_sb[:, 0:1]).then_inc(hThi_ready, 1)

            def take(key, dst, func, **more):
                i = nth[key]
                act.wait_ge(chunk_ready, i + 1)
                nc.scalar.activation(dst, wide[i % BANKS][:], func, **more).then_inc(chunk_taken, 1)

            def silus(kind, g, *chunks):
                dst = {"u": u, "z": z}[kind]
                for c in chunks:
                    take((kind, g, c), dst[:, g, c], ACT.Silu)

            def gates(g, *chunks):
                for c in chunks:
                    if g >= 2:
                        act.wait_ge(scan_done, B * (C * (g - 2) + c + 1))
                    take(("l", g, c), lam[:, g % 2, c], ACT.Sigmoid, bias=bdt_sb[:, c:c + 1])

            def x1_hi(g):
                act.wait_ge(x1T_ready, g + 1)
                if g >= 2:
                    act.wait_ge(chunk_ready, read_last("h", g - 2))
                nc.scalar.activation(x1T_hi[:, g % 2], turn[:], ACT.Copy).then_inc(x1hi_ready, 1)

            def gelus(g, *chunks):
                if g >= 2:
                    act.wait_ge(rows_ready, unit("y", g - 2, len(PIECES[g - 2]) - 1) + 1)
                for c in chunks:
                    take(("h", g, c), hid[:, g % 2, c], ACT.Gelu, scale=alpha1[:, c:c + 1], bias=b1_sb[:, c:c + 1])

            def layernorm2(g, i):
                act.wait_ge(shift2_ready, 1 + sorted(by_scalar).index((g, i)))
                a, b = PIECES[g][i]
                for j in range(a, b):
                    last = nc.scalar.activation(y[:, g, j], v2[:, g, j], ACT.Identity,
                                                scale=rstd2[:, g, j:j + 1], bias=shift2[:, g, j:j + 1])
                last.then_inc(y_ready[g][i], 1)

            nc.scalar.preload_act_table(ACT.Silu)
            act.wait_ge(win_in, 16)
            nc.scalar.activation(win_hi[:], win_sb[:], ACT.Copy).then_inc(winhi_ready, 1)
            act.wait_ge(wnorm_in, 16)
            norm_weight(0)
            silus("u", 0, 0, 1)
            silus("z", 0, 0)
            norm_weight(1)
            silus("z", 0, 1)
            nc.scalar.preload_act_table(ACT.Sigmoid)
            act.wait_ge(bdt_in, 16)
            gates(0, 0)
            act.wait_ge(w2T_in, 16)
            nc.scalar.activation(sign2[:], w2T_sb[:], ACT.Sign).then_inc(sign2_ready, 1)
            gates(0, 1)
            nc.scalar.preload_act_table(ACT.Silu)
            silus("u", 1, 0, 1)
            norm_weight(2)
            silus("z", 1, 0, 1)
            nc.scalar.preload_act_table(ACT.Sigmoid)
            gates(1, 0, 1)
            nc.scalar.preload_act_table(ACT.Silu)
            silus("u", 2, 0, 1)
            norm_weight(3)
            silus("z", 2, 0)
            nc.scalar.preload_act_table(ACT.Sigmoid)
            gates(2, 0, 1)
            nc.scalar.preload_act_table(ACT.Silu)
            act.wait_ge(w1T_in, 16)
            nc.scalar.activation(sign1[:], w1T_sb[:], ACT.Sign).then_inc(sign1_ready, 1)
            silus("u", 3, 0)
            silus("z", 2, 1)
            x1_hi(0)
            silus("u", 3, 1)
            silus("z", 3, 0, 1)
            nc.scalar.preload_act_table(ACT.Sigmoid)
            gates(3, 0, 1)
            nc.scalar.preload_act_table(ACT.Gelu)
            x1_hi(1)
            act.wait_ge(b1_in, 16)
            act.wait_ge(alpha1_ready, 1)
            gelus(0, 0, 1, 2, 3)
            gelus(1, 0, 1, 2, 3)
            x1_hi(2)
            gelus(2, 0)
            x1_hi(3)
            gelus(2, 1, 2, 3)
            gelus(3, 0, 1, 2)
            layernorm2(0, 1)
            gelus(3, 3)
            layernorm2(1, 0)
            layernorm2(2, 1)

        @block.tensor
        def _(pe):
            def turn_x(g):
                if g >= 1:
                    pe.wait_ge(hThi_ready, g)
                    pe.wait_ge(hTlo_ready, g)
                for j in range(J):
                    pe.wait_ge(xs_ready, J * g + j + 1)
                    last = nc.tensor.transpose(turn[:, j * P:(j + 1) * P], xs[:, g % 2, j], ident[:])
                last.then_inc(xT_ready, 1)

            def bank(key):
                i = nth[key]
                if i >= BANKS:
                    pe.wait_ge(chunk_taken, i - BANKS + 1)
                return wide[i % BANKS][:]

            def high_products(kind, g, c):
                e = "uz".index(kind) * INNER + c * P
                dst = bank((kind, g, c))
                nc.tensor.matmul(dst, win_lo[:, e:e + P], hT_hi[:, g % 2], start=True, stop=False)
                nc.tensor.matmul(dst, win_hi[:, e:e + P], hT_hi[:, g % 2], start=False, stop=False)

            def low_product(kind, g, c):
                e = "uz".index(kind) * INNER + c * P
                nc.tensor.matmul(wide[nth[kind, g, c] % BANKS][:], win_hi[:, e:e + P], hT_lo[:, g % 2],
                                 start=False, stop=True).then_inc(chunk_ready, 1)

            def project_in(kind, g, *chunks):
                pe.wait_ge(hThi_ready, g + 1)
                for c in chunks:
                    high_products(kind, g, c)
                    pe.wait_ge(hTlo_ready, g + 1)
                    low_product(kind, g, c)

            def project_first():
                pe.wait_ge(hThi_ready, 1)
                for kind, _, c in steps[:BANKS]:
                    high_products(kind, 0, c)
                pe.wait_ge(hTlo_ready, 1)
                for kind, _, c in steps[:BANKS]:
                    low_product(kind, 0, c)

            def project_gate(g, *chunks):
                pe.wait_ge(chunk_taken, read_last("u", g))
                for c in chunks:
                    dst = bank(("l", g, c))
                    for k in range(C):
                        last = nc.tensor.matmul(dst, wdt_sb[:, k, c * P:(c + 1) * P], u[:, g, k],
                                                start=(k == 0), stop=(k == C - 1))
                    last.then_inc(chunk_ready, 1)

            def free_rows(n):
                if n >= ROW_BANKS:
                    pe.wait_ge(rows_taken, n - ROW_BANKS + 1)

            def project_out(g):
                n = unit("s", g)
                pe.wait_ge(gated_ready, g + 1)
                free_rows(n)
                for j in range(J):
                    for k in range(C):
                        last = nc.tensor.matmul(rows[n % ROW_BANKS][:, j], gated[:, g % 2, k, j], wout_sb[:, k],
                                                start=(k == 0), stop=(k == C - 1))
                last.then_inc(rows_ready, 1)

            def turn_x1(g):
                pe.wait_ge(x1_ready, J * (g + 1))
                if g == 0:
                    pe.wait_ge(hThi_ready, G)
                    pe.wait_ge(hTlo_ready, G)
                else:
                    pe.wait_ge(x1hi_ready, g)
                    pe.wait_ge(x1lo_ready, g)
                for j in range(J):
                    last = nc.tensor.transpose(turn[:, j * P:(j + 1) * P], x1[:, g, j], ident[:])
                last.then_inc(x1T_ready, 1)

            def ffn_in(g, *chunks):
                pe.wait_ge(x1hi_ready, g + 1)
                for c in chunks:
                    dst = bank(("h", g, c))
                    w = sign1[:, c * P:(c + 1) * P]
                    nc.tensor.matmul(dst, w, x1T_hi[:, g % 2], start=True, stop=False)
                    pe.wait_ge(x1lo_ready, g + 1)
                    nc.tensor.matmul(dst, w, x1T_lo[:, g % 2], start=False, stop=True).then_inc(chunk_ready, 1)

            def ffn_out(g, *pieces):
                pe.wait_ge(chunk_taken, read_last("h", g))
                for piece in pieces:
                    n = unit("y", g, piece)
                    free_rows(n)
                    a, b = PIECES[g][piece]
                    for j in range(a, b):
                        for c in range(HC):
                            last = nc.tensor.matmul(rows[n % ROW_BANKS][:, j - a], hid[:, g % 2, c, j * P:(j + 1) * P],
                                                    bw2T[:, c], start=(c == 0), stop=(c == HC - 1))
                    last.then_inc(rows_ready, 1)

            def spread_scales():
                n = unit("a", 0)
                pe.wait_ge(ones_ready, 1)
                pe.wait_ge(diag2_ready, 1)
                free_rows(n)
                nc.tensor.matmul(rows[n % ROW_BANKS][:, 0], ones[:], diag2[:], start=True,
                                 stop=True).then_inc(rows_ready, 1)

            pe.wait_ge(ident_ready, 1)
            for i in range(WARM):
                nc.tensor.transpose(wide[0][:, 0:P], ident[:], ident[:])
            turn_x(0)
            pe.wait_ge(winhi_ready, 1)
            pe.wait_ge(winlo_ready, 1)
            project_first()
            turn_x(1)
            pe.wait_ge(wdt_in, 16)
            project_gate(0, 0, 1)
            spread_scales()
            project_in("u", 1, 0)
            turn_x(2)
            project_in("u", 1, 1)
            project_in("z", 1, 0, 1)
            project_gate(1, 0, 1)
            pe.wait_ge(wout_in, 16)
            project_out(0)
            project_in("u", 2, 0, 1)
            turn_x(3)
            project_in("z", 2, 0)
            project_gate(2, 0, 1)
            project_out(1)
            project_in("u", 3, 0)
            project_in("z", 2, 1)
            turn_x1(0)
            project_in("u", 3, 1)
            project_in("z", 3, 0, 1)
            project_gate(3, 0, 1)
            turn_x1(1)
            pe.wait_ge(sign1_ready, 1)
            ffn_in(0, 0, 1, 2, 3)
            project_out(2)
            ffn_in(1, 0, 1, 2, 3)
            pe.wait_ge(rows_taken, unit("a", 0) + 1)
            ffn_out(0, 0)
            project_out(3)
            turn_x1(2)
            ffn_out(0, 1)
            ffn_out(1, 0)
            ffn_in(2, 0, 1, 2, 3)
            turn_x1(3)
            ffn_out(1, 1)
            ffn_in(3, 0, 1, 2)
            ffn_out(2, 0)
            ffn_in(3, 3)
            ffn_out(2, 1)
            ffn_out(3, 0, 1, 2)

        @block.vector
        def _(dve):
            def mean_squares(g, a=0, b=J):
                dve.wait_ge(x_in[g], 16)
                for j in range(a, b):
                    if g or j >= 2:
                        dve.wait_ge(meansq_ready, J * g + j - 1)
                    nc.vector.tensor_tensor_reduce(square[:, j % 2], x_sb[:, g, j], x_sb[:, g, j], 1.0 / D, RMS_EPS,
                                                   ALU.mult, ALU.add, meansq[:, g, j:j + 1]).then_inc(meansq_ready, 1)

            def win_low():
                dve.wait_ge(win_in, 16)
                dve.wait_ge(winhi_ready, 1)
                nc.vector.tensor_tensor(win_lo[:], win_sb[:], win_hi[:].bitcast(F32),
                                        ALU.subtract).then_inc(winlo_ready, 1)

            def scale_rows(g, a=0, b=J):
                dve.wait_ge(rms_ready, J * g + b)
                if g >= 2:
                    dve.wait_ge(xT_ready, g - 1)
                nc.vector.tensor_tensor(xs[:, g % 2, a:b], x_sb[:, g, a:b],
                                        rms_inv[:, g, a:b, None].to_broadcast([P, b - a, D]),
                                        ALU.mult).then_inc(xs_ready, b - a)

            def norm_weight_low(g):
                dve.wait_ge(hThi_ready, g + 1)
                if g >= 2:
                    dve.wait_ge(chunk_ready, read_last("uz", g - 2))
                at = "d (p j) -> d j p"
                nc.vector.scalar_tensor_tensor(out=hT_lo[:, g % 2, :].rearrange(at, j=J),
                                               in0=turn[:].rearrange("d (j p) -> d j p", j=J),
                                               scalar=wnorm_sb[:, 0:1],
                                               in1=hT_hi[:, g % 2, :].bitcast(F32).rearrange(at, j=J),
                                               op0=ALU.mult, op1=ALU.subtract).then_inc(hTlo_ready, 1)

            def drive(g, *chunks):
                if g >= 2:
                    dve.wait_ge(gated_ready, g - 1)
                for c in chunks:
                    dve.wait_ge(chunk_taken, nth["l", g, c] + 1)
                    nc.vector.scalar_tensor_tensor(out=s[:, g % 2, c], in0=lam[:, g % 2, c], scalar=1.0, in1=u[:, g, c],
                                                   op0=ALU.subtract, op1=ALU.mult).then_inc(drive_ready, 1)

            def scan(g, *chunks):
                for c in chunks:
                    dve.wait_ge(drive_ready, C * g + c + 1)
                    for b in range(B):
                        at = slice(b * SEQ, (b + 1) * SEQ)
                        nc.vector.tensor_tensor_scan(s[:, g % 2, c, at], lam[:, g % 2, c, at], s[:, g % 2, c, at],
                                                     0.0, ALU.mult, ALU.subtract).then_inc(scan_done, 1)

            def gate_out(g):
                dve.wait_ge(scan_done, B * C * (g + 1))
                dve.wait_ge(chunk_taken, read_last("z", g))
                if g >= 2:
                    dve.wait_ge(rows_ready, unit("s", g - 2) + 1)
                at = "d c (p j) -> d c p j"
                nc.vector.tensor_tensor(gated[:, g % 2].rearrange("d c j p -> d c p j"), s[:, g % 2].rearrange(at, j=J),
                                        z[:, g].rearrange(at, j=J), ALU.mult).then_inc(gated_ready, 1)

            def statistics(v, stats, done, mv, g, tiles, ready):
                for j in tiles:
                    nc.vector.bn_stats(stats[:, g, j], v[:, g, j]).then_inc(done, 1)
                for j in tiles:
                    dve.wait_ge(done, J * g + j + 1)
                    nc.vector.bn_aggr(mv[:, g, j], stats[:, g, j]).then_inc(ready, 1)

            def residual1(g):
                n = unit("s", g)
                dve.wait_ge(rows_ready, n + 1)
                nc.vector.scalar_tensor_tensor(out=v1[:, g], in0=x_sb[:, g], scalar=2.0, in1=rows[n % ROW_BANKS][:],
                                               op0=ALU.mult, op1=ALU.add).then_inc(rows_taken, 1)
                dve.wait_ge(rows_taken, n + 1)
                statistics(v1, stats1, stats1_done, mv1, g, range(J), var1_ready)

            def layernorm1(g):
                dve.wait_ge(rstd1_ready, g + 1)
                for j in range(J):
                    nc.vector.tensor_scalar(x1[:, g, j], v1[:, g, j], mv1[:, g, j, 0:1], rstd1[:, g, j:j + 1],
                                            ALU.subtract, ALU.mult).then_inc(x1_ready, 1)

            def x1_lo(g):
                dve.wait_ge(x1hi_ready, g + 1)
                if g >= 2:
                    dve.wait_ge(chunk_ready, read_last("h", g - 2))
                nc.vector.tensor_tensor(x1T_lo[:, g % 2], turn[:], x1T_hi[:, g % 2].bitcast(F32),
                                        ALU.subtract).then_inc(x1lo_ready, 1)

            def add_b2(g):
                dve.wait_ge(x1_ready, J * (g + 1))
                nc.vector.tensor_tensor(x1b[:, g], x1[:, g], b2_sb[:, None, :].to_broadcast([P, J, D]),
                                        ALU.add).then_inc(x1b_ready, 1)

            def residual2(g, i):
                dve.wait_ge(x1b_ready, g + 1)
                n = unit("y", g, i)
                a, b = PIECES[g][i]
                dve.wait_ge(rows_ready, n + 1)
                nc.vector.tensor_tensor(v2[:, g, a:b], x1b[:, g, a:b], rows[n % ROW_BANKS][:, 0:b - a],
                                        ALU.add).then_inc(rows_taken, 1)
                dve.wait_ge(rows_taken, n + 1)
                statistics(v2, stats2, stats2_done, mv2, g, range(a, b), var2_ready)

            def layernorm2(g, i):
                dve.wait_ge(rstd2_ready, pieces_before[g] + i + 1)
                a, b = PIECES[g][i]
                for j in range(a, b):
                    last = nc.vector.tensor_scalar(y[:, g, j], v2[:, g, j], mv2[:, g, j, 0:1], rstd2[:, g, j:j + 1],
                                                   ALU.subtract, ALU.mult)
                last.then_inc(y_ready[g][i], 1)

            def scales_of_w1():
                dve.wait_ge(w1_in, 16)
                nc.vector.tensor_reduce(sum1[:], w1_sb[:], AX_X, ALU.add, apply_absolute_value=True).then_inc(sum1_ready, 1)
                dve.wait_ge(sum1_ready, 1)
                nc.vector.tensor_scalar(alpha1[:], sum1[:], 1.0 / D, None, ALU.mult).then_inc(alpha1_ready, 1)

            def sums_of_w2():
                dve.wait_ge(w2_in, 16)
                nc.vector.tensor_reduce(sum2[:], w2_sb[:], AX_X, ALU.add, apply_absolute_value=True).then_inc(sum2_ready, 1)
                dve.wait_ge(ident_ready, 1)
                dve.wait_ge(sum2_ready, 1)
                nc.vector.tensor_scalar(diag2[:], ident[:], sum2[:, 0:1], None, ALU.mult).then_inc(diag2_ready, 1)

            def binarise_w2():
                n = unit("a", 0)
                dve.wait_ge(rows_ready, n + 1)
                dve.wait_ge(sign2_ready, 1)
                nc.vector.scalar_tensor_tensor(out=bw2T[:], in0=sign2[:], scalar=1.0 / H,
                                               in1=rows[n % ROW_BANKS][:, 0:1].to_broadcast([P, HC, D]),
                                               op0=ALU.mult, op1=ALU.mult).then_inc(rows_taken, 1)

            mean_squares(0, 0, 2)
            mean_squares(0, 2, 4)
            scale_rows(0, 0, 2)
            scale_rows(0, 2, 4)
            win_low()
            mean_squares(1)
            dve.wait_ge(wnorm_in, 16)
            norm_weight_low(0)
            mean_squares(2)
            scale_rows(1)
            mean_squares(3)
            sums_of_w2()
            scale_rows(2)
            scale_rows(3)
            scales_of_w1()
            norm_weight_low(1)
            drive(0, 0)
            scan(0, 0)
            drive(0, 1)
            scan(0, 1)
            binarise_w2()
            gate_out(0)
            norm_weight_low(2)
            drive(1, 0)
            scan(1, 0)
            drive(1, 1)
            residual1(0)
            scan(1, 1)
            norm_weight_low(3)
            gate_out(1)
            layernorm1(0)
            drive(2, 0, 1)
            residual1(1)
            scan(2, 0, 1)
            layernorm1(1)
            x1_lo(0)
            gate_out(2)
            drive(3, 0, 1)
            x1_lo(1)
            scan(3, 0, 1)
            residual1(2)
            gate_out(3)
            dve.wait_ge(b2_in, 16)
            add_b2(0)
            layernorm1(2)
            residual2(0, 0)
            residual1(3)
            x1_lo(2)
            layernorm1(3)
            residual2(0, 1)
            add_b2(1)
            x1_lo(3)
            layernorm2(0, 0)
            add_b2(2)
            residual2(1, 0)
            residual2(1, 1)
            add_b2(3)
            residual2(2, 0)
            layernorm2(1, 1)
            residual2(2, 1)
            layernorm2(2, 0)
            residual2(3, 0)
            residual2(3, 1)
            residual2(3, 2)
            layernorm2(3, 0)
            layernorm2(3, 1)
            layernorm2(3, 2)

def kernel(L0_attn_x, L0_attn_w_norm, L0_attn_W_in, L0_attn_W_dt, L0_attn_b_dt, L0_attn_W_out,
           L0_ffn_w1, L0_ffn_b1, L0_ffn_w2, L0_ffn_b2):
    import numpy as _np
    import concourse.bacc as _bacc
    from concourse import mybir as _mybir
    from concourse.bass_utils import run_bass_kernel_spmd as _run

    def columns(v):
        return _np.asarray(v).reshape(-1, P).T

    shape = _np.asarray(L0_attn_x).shape
    laid_out = {
        "x": _np.asarray(L0_attn_x).reshape(-1, shape[-1]),
        "w_norm": columns(L0_attn_w_norm),
        "W_inT": _np.asarray(L0_attn_W_in).T,
        "W_dtT": _np.asarray(L0_attn_W_dt).T,
        "b_dt": columns(L0_attn_b_dt),
        "W_outT": _np.asarray(L0_attn_W_out).T,
        "w1": _np.asarray(L0_ffn_w1),
        "w1T": _np.asarray(L0_ffn_w1).T,
        "b1": columns(L0_ffn_b1),
        "w2": _np.asarray(L0_ffn_w2),
        "w2T": _np.asarray(L0_ffn_w2).T,
        "b2": _np.asarray(L0_ffn_b2).reshape(1, -1),
    }
    nc = _bacc.Bacc("TRN2", target_bir_lowering=False, num_devices=1)
    arrays, args = {}, []
    for name, a in laid_out.items():
        a = _np.ascontiguousarray(a)
        arrays[f"in_{name}"] = a
        args.append(nc.dram_tensor(f"in_{name}", a.shape, _mybir.dt.from_np(a.dtype), kind="ExternalInput").ap())
    args.append(nc.dram_tensor("out_y", laid_out["x"].shape, _mybir.dt.float32, kind="ExternalOutput").ap())
    gated_scan_then_binary_ffn(nc, *args)
    r = _run(nc, [arrays], core_ids=[0])
    return r.results[0]["out_y"].reshape(shape)
```

```python
from contextlib import ExitStack

import concourse.bass as bass
from concourse import mybir

ALU = mybir.AluOpType
ACT = mybir.ActivationFunctionType
AX_X = mybir.AxisListType.X
F32 = mybir.dt.float32
F32R = mybir.dt.float32r

P = 128
RMS_EPS = 1e-5
LN_EPS = 1e-5


def gated_scan_then_binary_ffn(nc, x, w_norm, W_inT, W_dtT, b_dt, W_outT, w1, w1T, b1, w2, w2T, b2, out):
    TOK, D = x.shape
    INNER = W_dtT.shape[0]
    H = w1T.shape[1]
    SEQ = 256
    GT = 512
    G = TOK // GT
    J = GT // P
    B = GT // SEQ
    C = INNER // P
    HC = H // P
    assert D == P and GT % SEQ == 0 and TOK % GT == 0

    steps = [("u", 0, 0), ("u", 0, 1), ("z", 0, 0), ("z", 0, 1), ("l", 0, 0), ("l", 0, 1), ("u", 1, 0),
             ("u", 1, 1), ("u", 2, 0), ("u", 2, 1), ("l", 1, 0), ("l", 1, 1), ("z", 1, 0), ("z", 1, 1),
             ("z", 2, 0), ("u", 3, 0), ("l", 2, 0), ("u", 3, 1), ("l", 2, 1), ("l", 3, 0), ("z", 2, 1),
             ("z", 3, 0), ("z", 3, 1), ("l", 3, 1), ("h", 0, 0), ("h", 0, 1), ("h", 0, 2), ("h", 0, 3),
             ("h", 1, 0), ("h", 1, 1), ("h", 1, 2), ("h", 1, 3), ("h", 2, 0), ("h", 2, 1), ("h", 2, 2),
             ("h", 2, 3), ("h", 3, 0), ("h", 3, 1), ("h", 3, 2), ("h", 3, 3)]
    nth = {step: i for i, step in enumerate(steps)}
    assert len(nth) == G * (3 * C + HC)
    BANKS = 4

    PIECES = [[(0, 4)], [(0, 4)], [(0, 2), (2, 4)], [(0, 2), (2, 3), (3, 4)]]
    STORES = [(g, [i]) for g in range(G - 1) for i in range(len(PIECES[g]))] + [(G - 1, [0]), (G - 1, [1, 2])]
    pieces_before = [sum(len(p) for p in PIECES[:g]) for g in range(G)]

    rows_order = [("s", 0, 0), ("s", 1, 0), ("a", 0, 0), ("s", 2, 0), ("y", 0, 0), ("s", 3, 0), ("y", 1, 0),
                  ("y", 2, 0), ("y", 2, 1), ("y", 3, 0), ("y", 3, 1), ("y", 3, 2)]
    assert len(rows_order) == G + 1 + sum(len(p) for p in PIECES)
    ROW_BANKS = 3
    JH = J // 2
    by_scalar = {(0, 0), (1, 0), (2, 1)}
    by_scalar1 = {0, 1, 2}
    squares_by_scalar = {2}
    split_gate = {2, 3}
    eps_by_vector = {(G - 1, 1), (G - 1, 2)}
    WARM = 16

    def unit(kind, g, piece=0):
        return rows_order.index((kind, g, piece))

    def read_last(kinds, g):
        return max(i for (kind, of, c), i in nth.items() if kind in kinds and of == g) + 1

    def in_time(hT, half=None):
        tiles = hT.rearrange("d (p j) -> d j p", j=J)
        return tiles if half is None else tiles[:, half * JH:(half + 1) * JH]

    with ExitStack() as ctx:
        def sb(name, shape, dt=F32):
            return ctx.enter_context(nc.sbuf_tensor(name, shape, dt))

        def ps(name, shape):
            return ctx.enter_context(nc.psum_tensor(name, shape, F32))

        def sem(name):
            return ctx.enter_context(nc.semaphore(name))

        wnorm_sb = sb("wnorm_sb", [P, 1])
        win_sb = sb("win_sb", [P, 2 * INNER])
        win_hi = sb("win_hi", [P, 2 * INNER], F32R)
        win_lo = sb("win_lo", [P, 2 * INNER], F32R)
        wdt_sb = sb("wdt_sb", [P, C, INNER])
        wout_sb = sb("wout_sb", [P, C, D])
        bdt_sb = sb("bdt_sb", [P, C])
        half_bdt = sb("half_bdt", [P, C])
        wdt_hi = sb("wdt_hi", [P, C, INNER], F32R)
        wdt_lo = sb("wdt_lo", [P, C, INNER], F32R)
        u_hi = sb("u_hi", [P, 2, C, GT], F32R)
        u_lo = sb("u_lo", [P, 2, C, GT], F32R)
        w1T_sb = sb("w1T_sb", [P, H])
        sign1 = sb("sign1", [P, H], F32R)
        w1_sb = sb("w1_sb", [P, HC, D])
        sum1 = sb("sum1", [P, HC])
        alpha1 = sb("alpha1", [P, HC])
        b1_sb = sb("b1_sb", [P, HC])
        w2T_sb = sb("w2T_sb", [P, HC, D])
        sign2 = sb("sign2", [P, HC, D])
        w2_sb = sb("w2_sb", [P, H])
        sum2 = sb("sum2", [P, 1])
        diag2 = sb("diag2", [P, D])
        bw2T = sb("bw2T", [P, HC, D])
        b2_sb = sb("b2_sb", [P, D])
        ident = sb("ident", [P, P])
        ones = sb("ones", [P, P])
        minus_half = sb("minus_half", [P, J])

        x_sb = sb("x_sb", [P, G, J, D])
        square = sb("square", [P, 2, D])
        square_s = sb("square_s", [P, 2, D])
        sumsq = sb("sumsq", [P, G, J])
        meansq = sb("meansq", [P, G, J])
        rms_inv = sb("rms_inv", [P, G, J])
        xs = sb("xs", [P, 2, J, D])
        hT_hi = sb("hT_hi", [P, 2, GT], F32R)
        hT_lo = sb("hT_lo", [P, 2, GT], F32R)
        u = sb("u", [P, G, C, GT])
        z = sb("z", [P, G, C, GT])
        lam = sb("lam", [P, 2, C, GT])
        s = sb("s", [P, 2, C, GT])
        gated = sb("gated", [P, 2, C, J, P])
        v1 = sb("v1", [P, G, J, D])
        stats1 = sb("stats1", [P, G, J, 6])
        stats2 = sb("stats2", [P, G, J, 6])
        mv1 = sb("mv1", [P, G, J, 2])
        vare1 = sb("vare1", [P, G, J])
        rstd1 = sb("rstd1", [P, G, J])
        minus_m1 = sb("minus_m1", [P, G, J])
        shift1 = sb("shift1", [P, G, J])
        x1 = sb("x1", [P, G, J, D])
        x1b = sb("x1b", [P, G, J, D])
        x1T_hi = sb("x1T_hi", [P, 2, GT], F32R)
        x1T_lo = sb("x1T_lo", [P, 2, GT], F32R)
        hid = sb("hid", [P, 2, HC, GT])
        v2 = sb("v2", [P, G, J, D])
        mv2 = sb("mv2", [P, G, J, 2])
        vare2 = sb("vare2", [P, G, J])
        rstd2 = sb("rstd2", [P, G, J])
        minus_m2 = sb("minus_m2", [P, G, J])
        shift2 = sb("shift2", [P, G, J])
        y = sb("y", [P, G, J, D])

        turn = ps("turn", [P, GT])
        rows = [ps(f"rows{i}", [P, J, D]) for i in range(ROW_BANKS)]
        turn_first = [turn[:, 0:JH * P], rows[ROW_BANKS - 1][:, 0:JH].rearrange("p j d -> p (j d)")]
        wide = [ps(f"wide{i}", [P, GT]) for i in range(BANKS)]

        x_in = [sem(f"x_in{g}") for g in range(G)]
        x_rest_in = sem("x_rest_in")
        wnorm_in, win_in, wdt_in, wout_in, bdt_in = (
            sem(n) for n in ("wnorm_in", "win_in", "wdt_in", "wout_in", "bdt_in"))
        w1_in, w1T_in, b1_in, w2_in, w2T_in, b2_in = (
            sem(n) for n in ("w1_in", "w1T_in", "b1_in", "w2_in", "w2T_in", "b2_in"))
        zeroed = sem("zeroed")
        ident_ready = sem("ident_ready")
        power_ready = sem("power_ready")
        ones_ready = sem("ones_ready")
        winhi_ready = sem("winhi_ready")
        winlo_ready = sem("winlo_ready")
        meansq_ready = sem("meansq_ready")
        sumsq_ready = sem("sumsq_ready")
        rms_ready = sem("rms_ready")
        xs_ready = [sem(f"xs_ready{g}") for g in range(G)]
        xT_first_ready = sem("xT_first_ready")
        xT_ready = sem("xT_ready")
        hThi_first_ready = sem("hThi_first_ready")
        hThi_ready = sem("hThi_ready")
        hTlo_first_ready = sem("hTlo_first_ready")
        hTlo_ready = sem("hTlo_ready")
        chunk_ready = sem("chunk_ready")
        chunk_taken = sem("chunk_taken")
        half_bdt_ready = sem("half_bdt_ready")
        lam_ready = [[sem(f"lam_ready{g}_{c}") for c in range(C)] for g in range(G)]
        wdthi_ready = sem("wdthi_ready")
        wdtlo_ready = sem("wdtlo_ready")
        uhi_ready = {g: [sem(f"uhi_ready{g}_{c}") for c in range(C)] for g in split_gate}
        ulo_ready = sem("ulo_ready")
        drive_ready = sem("drive_ready")
        scan_done = sem("scan_done")
        gated_ready = sem("gated_ready")
        rows_ready = sem("rows_ready")
        rows_taken = sem("rows_taken")
        stats1_done = sem("stats1_done")
        stats2_done = sem("stats2_done")
        var1_ready = sem("var1_ready")
        vare_ready = sem("vare_ready")
        vare2_ready = sem("vare2_ready")
        rstd1_ready = sem("rstd1_ready")
        x1_ready = [sem(f"x1_ready{g}") for g in range(G)]
        shift1_ready = sem("shift1_ready")
        x1b_ready = sem("x1b_ready")
        x1T_ready = sem("x1T_ready")
        x1hi_ready = sem("x1hi_ready")
        x1lo_ready = sem("x1lo_ready")
        sign1_ready = sem("sign1_ready")
        sign2_ready = sem("sign2_ready")
        sum1_ready = sem("sum1_ready")
        sum2_ready = sem("sum2_ready")
        diag2_ready = sem("diag2_ready")
        alpha1_ready = sem("alpha1_ready")
        var2_ready = sem("var2_ready")
        rstd2_ready = sem("rstd2_ready")
        minus_m_ready = sem("minus_m_ready")
        shift2_ready = sem("shift2_ready")
        y_ready = [[sem(f"y_ready{g}_{i}") for i in range(len(PIECES[g]))] for g in range(G)]
        stored = sem("stored")

        block = ctx.enter_context(nc.Block())

        x_dram = x.rearrange("(g p j) d -> g p j d", p=P, j=J)
        out_dram = out.rearrange("(g p j) d -> g p j d", p=P, j=J)

        @block.sync
        def _(sp):
            def load_x(g):
                sp.dma_start(x_sb[:, g], x_dram[g]).then_inc(x_in[g], 16)

            sp.dma_start(x_sb[:, 0, 0:JH], x_dram[0][:, 0:JH]).then_inc(x_in[0], 16)
            sp.dma_start(x_sb[:, 0, JH:J], x_dram[0][:, JH:J]).then_inc(x_rest_in, 16)
            sp.dma_start(win_sb[:], W_inT).then_inc(win_in, 16)
            sp.dma_start(wnorm_sb[:], w_norm).then_inc(wnorm_in, 16)
            load_x(1)
            load_x(2)
            sp.dma_start(wdt_sb[:], W_dtT.rearrange("(c p) n -> p c n", p=P)).then_inc(wdt_in, 16)
            load_x(3)
            sp.dma_start(bdt_sb[:], b_dt).then_inc(bdt_in, 16)
            sp.dma_start(wout_sb[:], W_outT.rearrange("(c p) n -> p c n", p=P)).then_inc(wout_in, 16)
            sp.dma_start(w2T_sb[:], w2T.rearrange("(c p) d -> p c d", p=P)).then_inc(w2T_in, 16)
            sp.dma_start(w1T_sb[:], w1T).then_inc(w1T_in, 16)
            sp.dma_start(w1_sb[:], w1.rearrange("(c p) d -> p c d", p=P)).then_inc(w1_in, 16)
            sp.dma_start(w2_sb[:], w2).then_inc(w2_in, 16)
            sp.dma_start(b1_sb[:], b1).then_inc(b1_in, 16)
            sp.dma_start(b2_sb[:], b2.to_broadcast([P, D])).then_inc(b2_in, 16)
            for n, (g, pieces) in enumerate(STORES):
                for i in pieces:
                    sp.wait_ge(y_ready[g][i], 1)
                a, b = PIECES[g][pieces[0]][0], PIECES[g][pieces[-1]][1]
                sp.dma_start(out_dram[g][:, a:b], y[:, g, a:b]).then_inc(stored, 16)
            sp.wait_ge(stored, 16 * len(STORES))

        @block.gpsimd
        def _(pool):
            nc.gpsimd.memset(ident[:], 0.0).then_inc(zeroed, 1)
            nc.gpsimd.memset(minus_half[:], -0.5).then_inc(power_ready, 1)
            pool.wait_ge(zeroed, 1)
            nc.gpsimd.affine_select(out=ident[:], in_=ident[:], compare_op=ALU.not_equal, fill=1.0, base=0,
                                    pattern=[[-1, P]], channel_multiplier=1).then_inc(ident_ready, 1)
            nc.gpsimd.memset(ones[:], 1.0).then_inc(ones_ready, 1)
            pool.wait_ge(power_ready, 1)

            def inverse_rms(g, a, b):
                nonlocal roots
                if g in squares_by_scalar:
                    pool.wait_ge(sumsq_ready, J * (1 + sorted(squares_by_scalar).index(g)))
                    nc.gpsimd.tensor_scalar(meansq[:, g], sumsq[:, g], 1.0 / D, RMS_EPS, ALU.mult,
                                            ALU.add).then_inc(vare_ready, 1)
                    roots += 1
                    pool.wait_ge(vare_ready, roots)
                else:
                    by_vector = [k for k in range(g + 1) if k not in squares_by_scalar]
                    pool.wait_ge(meansq_ready, J * (len(by_vector) - 1) + b)
                nc.gpsimd.tensor_tensor(rms_inv[:, g, a:b], meansq[:, g, a:b], minus_half[:, a:b],
                                        ALU.pow).then_inc(rms_ready, b - a)

            def inverse_root(dst, mid, var, ready):
                nonlocal roots
                nc.gpsimd.tensor_scalar(mid, var, LN_EPS, None, ALU.add).then_inc(vare_ready, 1)
                roots += 1
                pool.wait_ge(vare_ready, roots)
                nc.gpsimd.tensor_tensor(dst, mid, minus_half[:, 0:dst.shape[1]], ALU.pow).then_inc(ready, 1)

            roots = 0

            def negate(dst, mean):
                nc.gpsimd.tensor_scalar(dst, mean, -1.0, None, ALU.mult).then_inc(minus_m_ready, 1)

            def shift(dst, minus_m, rstd, rstd_ready, n, ready):
                nonlocal shifts
                shifts += 1
                pool.wait_ge(minus_m_ready, shifts)
                pool.wait_ge(rstd_ready, n)
                nc.gpsimd.tensor_tensor(dst, minus_m, rstd, ALU.mult).then_inc(ready, 1)

            def inverse_deviation1(g):
                pool.wait_ge(var1_ready, J * (g + 1))
                if g in by_scalar1:
                    negate(minus_m1[:, g], mv1[:, g, :, 0])
                inverse_root(rstd1[:, g], vare1[:, g], mv1[:, g, :, 1], rstd1_ready)
                if g in by_scalar1:
                    shift(shift1[:, g], minus_m1[:, g], rstd1[:, g], rstd1_ready, g + 1, shift1_ready)

            def inverse_deviation2(g, i):
                a, b = PIECES[g][i]
                pool.wait_ge(var2_ready, J * g + b)
                if (g, i) in by_scalar:
                    negate(minus_m2[:, g, a:b], mv2[:, g, a:b, 0])
                if (g, i) in eps_by_vector:
                    pool.wait_ge(vare2_ready, 1 + sorted(eps_by_vector).index((g, i)))
                    nc.gpsimd.tensor_tensor(rstd2[:, g, a:b], vare2[:, g, a:b], minus_half[:, a:b],
                                            ALU.pow).then_inc(rstd2_ready, 1)
                else:
                    inverse_root(rstd2[:, g, a:b], vare2[:, g, a:b], mv2[:, g, a:b, 1], rstd2_ready)
                if (g, i) in by_scalar:
                    shift(shift2[:, g, a:b], minus_m2[:, g, a:b], rstd2[:, g, a:b], rstd2_ready,
                          pieces_before[g] + i + 1, shift2_ready)

            shifts = 0

            inverse_rms(0, 0, 2)
            inverse_rms(0, 2, 4)
            inverse_rms(1, 0, J)
            inverse_rms(2, 0, J)
            inverse_rms(3, 0, J)
            inverse_deviation1(0)
            inverse_deviation1(1)
            inverse_deviation1(2)
            inverse_deviation2(0, 0)
            inverse_deviation1(3)
            inverse_deviation2(1, 0)
            inverse_deviation2(2, 0)
            inverse_deviation2(2, 1)
            inverse_deviation2(3, 0)
            inverse_deviation2(3, 1)
            inverse_deviation2(3, 2)

        @block.scalar
        def _(act):
            def norm_weight(g):
                act.wait_ge(xT_ready, g + 1)
                if g >= 2:
                    act.wait_ge(chunk_ready, read_last("uz", g - 2))
                nc.scalar.activation(in_time(hT_hi[:, g % 2]), turn[:].rearrange("d (j p) -> d j p", j=J),
                                     ACT.Copy, scale=wnorm_sb[:, 0:1]).then_inc(hThi_ready, 1)

            def norm_weight_first(half):
                act.wait_ge([xT_first_ready, xT_ready][half], 1)
                nc.scalar.activation(in_time(hT_hi[:, 0], half), turn_first[half].rearrange("d (j p) -> d j p", j=JH),
                                     ACT.Copy, scale=wnorm_sb[:, 0:1]).then_inc([hThi_first_ready, hThi_ready][half], 1)

            def take(key, dst, func, **more):
                i = nth[key]
                act.wait_ge(chunk_ready, i + 1)
                nc.scalar.activation(dst, wide[i % BANKS][:], func, **more).then_inc(chunk_taken, 1)

            def silus(kind, g, *chunks):
                dst = {"u": u, "z": z}[kind]
                for c in chunks:
                    take((kind, g, c), dst[:, g, c], ACT.Silu)

            def gates(g, *chunks):
                for c in chunks:
                    if g >= 2:
                        act.wait_ge(scan_done, B * (C * (g - 2) + c + 1))
                    take(("l", g, c), lam[:, g % 2, c], ACT.Tanh, scale=0.5, bias=half_bdt[:, c:c + 1])

            def lambdas(g, *chunks):
                for c in chunks:
                    act.wait_ge(chunk_taken, nth["l", g, c] + 1)
                    nc.scalar.activation(lam[:, g % 2, c], lam[:, g % 2, c], ACT.Copy, bias=0.5,
                                         scale=0.5).then_inc(lam_ready[g][c], 1)

            def sums_of_squares(g):
                act.wait_ge(x_in[g], 16)
                n = J * sorted(squares_by_scalar).index(g)
                for j in range(J):
                    if n + j >= 2:
                        act.wait_ge(sumsq_ready, n + j - 1)
                    nc.scalar.activation(square_s[:, j % 2], x_sb[:, g, j], ACT.Square,
                                         accum_out=sumsq[:, g, j:j + 1]).then_inc(sumsq_ready, 1)

            def scale_rows(g):
                act.wait_ge(rms_ready, J * (g + 1))
                if g >= 2:
                    act.wait_ge(xT_ready, g - 1)
                for j in range(J):
                    nc.scalar.activation(xs[:, g % 2, j], x_sb[:, g, j], ACT.Copy,
                                         scale=rms_inv[:, g, j:j + 1]).then_inc(xs_ready[g], 1)

            def layernorm1(g, half):
                act.wait_ge(shift1_ready, 1 + sorted(by_scalar1).index(g))
                for j in range(half * J // 2, (half + 1) * J // 2):
                    nc.scalar.activation(x1[:, g, j], v1[:, g, j], ACT.Identity, scale=rstd1[:, g, j:j + 1],
                                         bias=shift1[:, g, j:j + 1]).then_inc(x1_ready[g], 1)

            def u_high(g, c):
                act.wait_ge(chunk_taken, nth["u", g, c] + 1)
                if g - 2 in split_gate:
                    act.wait_ge(chunk_ready, read_last("l", g - 2))
                nc.scalar.activation(u_hi[:, g % 2, c], u[:, g, c], ACT.Copy).then_inc(uhi_ready[g][c], 1)

            def x1_hi(g):
                act.wait_ge(x1T_ready, g + 1)
                if g >= 2:
                    act.wait_ge(chunk_ready, read_last("h", g - 2))
                nc.scalar.activation(x1T_hi[:, g % 2], turn[:], ACT.Copy).then_inc(x1hi_ready, 1)

            def gelus(g, *chunks):
                if g >= 2:
                    act.wait_ge(rows_ready, unit("y", g - 2, len(PIECES[g - 2]) - 1) + 1)
                for c in chunks:
                    take(("h", g, c), hid[:, g % 2, c], ACT.Gelu, scale=alpha1[:, c:c + 1], bias=b1_sb[:, c:c + 1])

            def layernorm2(g, i):
                act.wait_ge(shift2_ready, 1 + sorted(by_scalar).index((g, i)))
                a, b = PIECES[g][i]
                for j in range(a, b):
                    last = nc.scalar.activation(y[:, g, j], v2[:, g, j], ACT.Identity,
                                                scale=rstd2[:, g, j:j + 1], bias=shift2[:, g, j:j + 1])
                last.then_inc(y_ready[g][i], 1)

            nc.scalar.preload_act_table(ACT.Silu)
            act.wait_ge(win_in, 16)
            nc.scalar.activation(win_hi[:], win_sb[:], ACT.Copy).then_inc(winhi_ready, 1)
            act.wait_ge(wnorm_in, 16)
            norm_weight_first(0)
            norm_weight_first(1)
            sums_of_squares(2)
            act.wait_ge(bdt_in, 16)
            nc.scalar.activation(half_bdt[:], bdt_sb[:], ACT.Copy, scale=0.5).then_inc(half_bdt_ready, 1)
            silus("u", 0, 0, 1)
            norm_weight(1)
            silus("z", 0, 0)
            act.wait_ge(wdt_in, 16)
            nc.scalar.activation(wdt_hi[:], wdt_sb[:], ACT.Copy).then_inc(wdthi_ready, 1)
            silus("z", 0, 1)
            act.wait_ge(half_bdt_ready, 1)
            gates(0, 0)
            norm_weight(2)
            scale_rows(3)
            gates(0, 1)
            silus("u", 1, 0)
            lambdas(0, 1)
            silus("u", 1, 1)
            silus("u", 2, 0, 1)
            u_high(2, 0)
            u_high(2, 1)
            gates(1, 0)
            lambdas(1, 0)
            gates(1, 1)
            silus("z", 1, 0)
            lambdas(1, 1)
            norm_weight(3)
            silus("z", 1, 1)
            act.wait_ge(w1T_in, 16)
            nc.scalar.activation(sign1[:], w1T_sb[:], ACT.Sign).then_inc(sign1_ready, 1)
            silus("z", 2, 0)
            act.wait_ge(w2T_in, 16)
            nc.scalar.activation(sign2[:], w2T_sb[:], ACT.Sign).then_inc(sign2_ready, 1)
            silus("u", 3, 0)
            u_high(3, 0)
            gates(2, 0)
            silus("u", 3, 1)
            lambdas(2, 0)
            u_high(3, 1)
            layernorm1(0, 0)
            gates(2, 1)
            layernorm1(0, 1)
            lambdas(2, 1)
            gates(3, 0)
            x1_hi(0)
            lambdas(3, 0)
            silus("z", 2, 1)
            silus("z", 3, 0, 1)
            layernorm1(1, 1)
            gates(3, 1)
            nc.scalar.preload_act_table(ACT.Gelu)
            act.wait_ge(b1_in, 16)
            act.wait_ge(alpha1_ready, 1)
            gelus(0, 0)
            x1_hi(1)
            gelus(0, 1, 2, 3)
            lambdas(3, 1)
            gelus(1, 0, 1, 2)
            layernorm1(2, 0)
            layernorm1(2, 1)
            x1_hi(2)
            gelus(1, 3)
            gelus(2, 0, 1, 2)
            layernorm2(0, 0)
            gelus(2, 3)
            x1_hi(3)
            gelus(3, 0, 1, 2, 3)
            layernorm2(1, 0)
            layernorm2(2, 1)

        @block.tensor
        def _(pe):
            def turn_x(g):
                pe.wait_ge(hThi_ready, g)
                pe.wait_ge(hTlo_ready, g)
                for j in range(J):
                    pe.wait_ge(xs_ready[g], j + 1)
                    last = nc.tensor.transpose(turn[:, j * P:(j + 1) * P], xs[:, g % 2, j], ident[:])
                last.then_inc(xT_ready, 1)

            def turn_x_first(half):
                for i in range(JH):
                    j = half * JH + i
                    pe.wait_ge(xs_ready[0], j + 1)
                    last = nc.tensor.transpose(turn_first[half][:, i * P:(i + 1) * P], xs[:, 0, j], ident[:])
                last.then_inc([xT_first_ready, xT_ready][half], 1)

            def bank(key):
                i = nth[key]
                if i >= BANKS:
                    pe.wait_ge(chunk_taken, i - BANKS + 1)
                return wide[i % BANKS][:]

            def high_products(kind, g, c, half=None):
                e = "uz".index(kind) * INNER + c * P
                dst, h = bank((kind, g, c)), hT_hi[:, g % 2]
                if half is not None:
                    at = slice(half * JH, (half + 1) * JH)
                    dst, h = (a.rearrange("d (p j) -> d p j", j=J)[:, :, at] for a in (dst, h))
                nc.tensor.matmul(dst, win_lo[:, e:e + P], h, start=(half != 1), stop=False)
                nc.tensor.matmul(dst, win_hi[:, e:e + P], h, start=False, stop=False)

            def low_product(kind, g, c):
                e = "uz".index(kind) * INNER + c * P
                nc.tensor.matmul(wide[nth[kind, g, c] % BANKS][:], win_hi[:, e:e + P], hT_lo[:, g % 2],
                                 start=False, stop=True).then_inc(chunk_ready, 1)

            def project_in(kind, g, *chunks):
                pe.wait_ge(hThi_ready, g + 1)
                for c in chunks:
                    high_products(kind, g, c)
                    pe.wait_ge(hTlo_ready, g + 1)
                    low_product(kind, g, c)

            def project_first_high(kind, *halves):
                for half in halves:
                    pe.wait_ge([hThi_first_ready, hThi_ready][half], 1)
                    for c in range(C):
                        high_products(kind, 0, c, half)

            def project_first_low(kind, *chunks):
                pe.wait_ge(hTlo_first_ready, 1)
                pe.wait_ge(hTlo_ready, 1)
                for c in chunks:
                    low_product(kind, 0, c)

            def project_gate_by_parts(g, *chunks):
                for c in range(C):
                    pe.wait_ge(uhi_ready[g][c], 1)
                for c in chunks:
                    dst = bank(("l", g, c))
                    at = slice(c * P, (c + 1) * P)
                    for k in range(C):
                        nc.tensor.matmul(dst, wdt_lo[:, k, at], u_hi[:, g % 2, k], start=(k == 0), stop=False)
                        nc.tensor.matmul(dst, wdt_hi[:, k, at], u_hi[:, g % 2, k], start=False, stop=False)
                    for k in range(C):
                        pe.wait_ge(ulo_ready, C * sorted(split_gate).index(g) + k + 1)
                        last = nc.tensor.matmul(dst, wdt_hi[:, k, at], u_lo[:, g % 2, k], start=False, stop=(k == C - 1))
                    last.then_inc(chunk_ready, 1)

            def project_gate(g, *chunks):
                pe.wait_ge(chunk_taken, read_last("u", g))
                for c in chunks:
                    dst = bank(("l", g, c))
                    for k in range(C):
                        last = nc.tensor.matmul(dst, wdt_sb[:, k, c * P:(c + 1) * P], u[:, g, k],
                                                start=(k == 0), stop=(k == C - 1))
                    last.then_inc(chunk_ready, 1)

            def free_rows(n):
                if n >= ROW_BANKS:
                    pe.wait_ge(rows_taken, n - ROW_BANKS + 1)

            def project_out(g):
                n = unit("s", g)
                pe.wait_ge(gated_ready, g + 1)
                free_rows(n)
                for j in range(J):
                    for k in range(C):
                        last = nc.tensor.matmul(rows[n % ROW_BANKS][:, j], gated[:, g % 2, k, j], wout_sb[:, k],
                                                start=(k == 0), stop=(k == C - 1))
                last.then_inc(rows_ready, 1)

            def turn_x1(g):
                pe.wait_ge(x1_ready[g], J)
                if g == 0:
                    pe.wait_ge(hThi_ready, G)
                    pe.wait_ge(hTlo_ready, G)
                else:
                    pe.wait_ge(x1hi_ready, g)
                    pe.wait_ge(x1lo_ready, g)
                for j in range(J):
                    last = nc.tensor.transpose(turn[:, j * P:(j + 1) * P], x1[:, g, j], ident[:])
                last.then_inc(x1T_ready, 1)

            def ffn_in(g, *chunks):
                pe.wait_ge(x1hi_ready, g + 1)
                for c in chunks:
                    dst = bank(("h", g, c))
                    w = sign1[:, c * P:(c + 1) * P]
                    nc.tensor.matmul(dst, w, x1T_hi[:, g % 2], start=True, stop=False)
                    pe.wait_ge(x1lo_ready, g + 1)
                    nc.tensor.matmul(dst, w, x1T_lo[:, g % 2], start=False, stop=True).then_inc(chunk_ready, 1)

            def ffn_out(g, *pieces):
                pe.wait_ge(chunk_taken, read_last("h", g))
                for piece in pieces:
                    n = unit("y", g, piece)
                    free_rows(n)
                    a, b = PIECES[g][piece]
                    for j in range(a, b):
                        for c in range(HC):
                            last = nc.tensor.matmul(rows[n % ROW_BANKS][:, j - a], hid[:, g % 2, c, j * P:(j + 1) * P],
                                                    bw2T[:, c], start=(c == 0), stop=(c == HC - 1))
                    last.then_inc(rows_ready, 1)

            def spread_scales():
                n = unit("a", 0)
                pe.wait_ge(ones_ready, 1)
                pe.wait_ge(diag2_ready, 1)
                free_rows(n)
                nc.tensor.matmul(rows[n % ROW_BANKS][:, 0], ones[:], diag2[:], start=True,
                                 stop=True).then_inc(rows_ready, 1)

            pe.wait_ge(ident_ready, 1)
            for i in range(WARM):
                nc.tensor.transpose(wide[0][:, 0:P], ident[:], ident[:])
            turn_x_first(0)
            turn_x_first(1)
            pe.wait_ge(winhi_ready, 1)
            pe.wait_ge(winlo_ready, 1)
            project_first_high("u", 0, 1)
            project_first_high("z", 0)
            project_first_low("u", 0, 1)
            project_first_high("z", 1)
            project_first_low("z", 0)
            turn_x(1)
            project_first_low("z", 1)
            pe.wait_ge(wdt_in, 16)
            project_gate(0, 0)
            turn_x(2)
            project_gate(0, 1)
            project_in("u", 1, 0, 1)
            turn_x(3)
            project_in("u", 2, 0, 1)
            project_gate(1, 0, 1)
            project_in("z", 1, 0, 1)
            project_in("z", 2, 0)
            pe.wait_ge(wout_in, 16)
            project_out(0)
            project_in("u", 3, 0)
            pe.wait_ge(wdthi_ready, 1)
            pe.wait_ge(wdtlo_ready, 1)
            project_gate_by_parts(2, 0)
            project_in("u", 3, 1)
            project_gate_by_parts(2, 1)
            project_out(1)
            project_gate_by_parts(3, 0)
            turn_x1(0)
            project_in("z", 2, 1)
            project_in("z", 3, 0, 1)
            project_gate_by_parts(3, 1)
            pe.wait_ge(sign1_ready, 1)
            ffn_in(0, 0, 1)
            turn_x1(1)
            spread_scales()
            ffn_in(0, 2)
            project_out(2)
            ffn_in(0, 3)
            ffn_in(1, 0, 1, 2)
            pe.wait_ge(rows_taken, unit("a", 0) + 1)
            ffn_out(0, 0)
            ffn_in(1, 3)
            turn_x1(2)
            project_out(3)
            ffn_in(2, 0, 1, 2, 3)
            ffn_out(1, 0)
            turn_x1(3)
            ffn_out(2, 0)
            ffn_in(3, 0, 1, 2, 3)
            ffn_out(2, 1)
            ffn_out(3, 0, 1, 2)

        @block.vector
        def _(dve):
            def mean_squares(g, a=0, b=J):
                dve.wait_ge(x_rest_in if g == 0 and a > 0 else x_in[g], 16)
                n = J * len([k for k in range(g) if k not in squares_by_scalar])
                for j in range(a, b):
                    if n + j >= 2:
                        dve.wait_ge(meansq_ready, n + j - 1)
                    nc.vector.tensor_tensor_reduce(square[:, j % 2], x_sb[:, g, j], x_sb[:, g, j], 1.0 / D, RMS_EPS,
                                                   ALU.mult, ALU.add, meansq[:, g, j:j + 1]).then_inc(meansq_ready, 1)

            def win_low():
                dve.wait_ge(win_in, 16)
                dve.wait_ge(winhi_ready, 1)
                nc.vector.tensor_tensor(win_lo[:], win_sb[:], win_hi[:].bitcast(F32),
                                        ALU.subtract).then_inc(winlo_ready, 1)

            def scale_rows(g, a=0, b=J):
                dve.wait_ge(rms_ready, J * g + b)
                if g >= 2:
                    dve.wait_ge(xT_ready, g - 1)
                nc.vector.tensor_tensor(xs[:, g % 2, a:b], x_sb[:, g, a:b],
                                        rms_inv[:, g, a:b, None].to_broadcast([P, b - a, D]),
                                        ALU.mult).then_inc(xs_ready[g], b - a)

            def norm_weight_low(g):
                dve.wait_ge(hThi_ready, g + 1)
                if g >= 2:
                    dve.wait_ge(chunk_ready, read_last("uz", g - 2))
                nc.vector.scalar_tensor_tensor(out=in_time(hT_lo[:, g % 2]),
                                               in0=turn[:].rearrange("d (j p) -> d j p", j=J),
                                               scalar=wnorm_sb[:, 0:1], in1=in_time(hT_hi[:, g % 2].bitcast(F32)),
                                               op0=ALU.mult, op1=ALU.subtract).then_inc(hTlo_ready, 1)

            def norm_weight_low_first(half):
                dve.wait_ge([hThi_first_ready, hThi_ready][half], 1)
                nc.vector.scalar_tensor_tensor(out=in_time(hT_lo[:, 0], half),
                                               in0=turn_first[half].rearrange("d (j p) -> d j p", j=JH),
                                               scalar=wnorm_sb[:, 0:1], in1=in_time(hT_hi[:, 0].bitcast(F32), half),
                                               op0=ALU.mult, op1=ALU.subtract
                                               ).then_inc([hTlo_first_ready, hTlo_ready][half], 1)

            def lambdas(g, *chunks):
                for c in chunks:
                    dve.wait_ge(chunk_taken, nth["l", g, c] + 1)
                    nc.vector.tensor_scalar(lam[:, g % 2, c], lam[:, g % 2, c], 0.5, 0.5, ALU.mult,
                                            ALU.add).then_inc(lam_ready[g][c], 1)

            def u_high(g, c):
                dve.wait_ge(chunk_taken, nth["u", g, c] + 1)
                if g - 2 in split_gate:
                    dve.wait_ge(chunk_ready, read_last("l", g - 2))
                nc.vector.tensor_copy(u_hi[:, g % 2, c], u[:, g, c]).then_inc(uhi_ready[g][c], 1)

            def u_low(g, *chunks):
                for c in chunks:
                    dve.wait_ge(uhi_ready[g][c], 1)
                    if g - 2 in split_gate:
                        dve.wait_ge(chunk_ready, read_last("l", g - 2))
                    nc.vector.tensor_tensor(u_lo[:, g % 2, c], u[:, g, c], u_hi[:, g % 2, c].bitcast(F32),
                                            ALU.subtract).then_inc(ulo_ready, 1)

            def wdt_low():
                dve.wait_ge(wdt_in, 16)
                dve.wait_ge(wdthi_ready, 1)
                nc.vector.tensor_tensor(wdt_lo[:], wdt_sb[:], wdt_hi[:].bitcast(F32),
                                        ALU.subtract).then_inc(wdtlo_ready, 1)

            def drive(g, *chunks):
                if g >= 2:
                    dve.wait_ge(gated_ready, g - 1)
                for c in chunks:
                    dve.wait_ge(lam_ready[g][c], 1)
                    nc.vector.scalar_tensor_tensor(out=s[:, g % 2, c], in0=lam[:, g % 2, c], scalar=1.0, in1=u[:, g, c],
                                                   op0=ALU.subtract, op1=ALU.mult).then_inc(drive_ready, 1)

            def scan(g, *chunks):
                for c in chunks:
                    dve.wait_ge(drive_ready, C * g + c + 1)
                    for b in range(B):
                        at = slice(b * SEQ, (b + 1) * SEQ)
                        nc.vector.tensor_tensor_scan(s[:, g % 2, c, at], lam[:, g % 2, c, at], s[:, g % 2, c, at],
                                                     0.0, ALU.mult, ALU.subtract).then_inc(scan_done, 1)

            def gate_out(g):
                dve.wait_ge(scan_done, B * C * (g + 1))
                dve.wait_ge(chunk_taken, read_last("z", g))
                if g >= 2:
                    dve.wait_ge(rows_ready, unit("s", g - 2) + 1)
                at = "d c (p j) -> d c p j"
                nc.vector.tensor_tensor(gated[:, g % 2].rearrange("d c j p -> d c p j"), s[:, g % 2].rearrange(at, j=J),
                                        z[:, g].rearrange(at, j=J), ALU.mult).then_inc(gated_ready, 1)

            def statistics(v, stats, done, mv, g, tiles, ready):
                for j in tiles:
                    nc.vector.bn_stats(stats[:, g, j], v[:, g, j]).then_inc(done, 1)
                for j in tiles:
                    dve.wait_ge(done, J * g + j + 1)
                    nc.vector.bn_aggr(mv[:, g, j], stats[:, g, j]).then_inc(ready, 1)

            def residual1(g):
                n = unit("s", g)
                dve.wait_ge(rows_ready, n + 1)
                nc.vector.scalar_tensor_tensor(out=v1[:, g], in0=x_sb[:, g], scalar=2.0, in1=rows[n % ROW_BANKS][:],
                                               op0=ALU.mult, op1=ALU.add).then_inc(rows_taken, 1)
                dve.wait_ge(rows_taken, n + 1)
                statistics(v1, stats1, stats1_done, mv1, g, range(J), var1_ready)

            def layernorm1(g, half):
                dve.wait_ge(rstd1_ready, g + 1)
                for j in range(half * J // 2, (half + 1) * J // 2):
                    nc.vector.tensor_scalar(x1[:, g, j], v1[:, g, j], mv1[:, g, j, 0:1], rstd1[:, g, j:j + 1],
                                            ALU.subtract, ALU.mult).then_inc(x1_ready[g], 1)

            def x1_lo(g):
                dve.wait_ge(x1hi_ready, g + 1)
                if g >= 2:
                    dve.wait_ge(chunk_ready, read_last("h", g - 2))
                nc.vector.tensor_tensor(x1T_lo[:, g % 2], turn[:], x1T_hi[:, g % 2].bitcast(F32),
                                        ALU.subtract).then_inc(x1lo_ready, 1)

            def add_b2(g):
                dve.wait_ge(x1_ready[g], J)
                nc.vector.tensor_tensor(x1b[:, g], x1[:, g], b2_sb[:, None, :].to_broadcast([P, J, D]),
                                        ALU.add).then_inc(x1b_ready, 1)

            def residual2(g, i):
                dve.wait_ge(x1b_ready, g + 1)
                n = unit("y", g, i)
                a, b = PIECES[g][i]
                dve.wait_ge(rows_ready, n + 1)
                nc.vector.tensor_tensor(v2[:, g, a:b], x1b[:, g, a:b], rows[n % ROW_BANKS][:, 0:b - a],
                                        ALU.add).then_inc(rows_taken, 1)
                dve.wait_ge(rows_taken, n + 1)
                statistics(v2, stats2, stats2_done, mv2, g, range(a, b), var2_ready)
                if (g, i) in eps_by_vector:
                    dve.wait_ge(var2_ready, J * g + b)
                    nc.vector.tensor_scalar(vare2[:, g, a:b], mv2[:, g, a:b, 1], LN_EPS, None,
                                            ALU.add).then_inc(vare2_ready, 1)

            def layernorm2(g, i):
                dve.wait_ge(rstd2_ready, pieces_before[g] + i + 1)
                a, b = PIECES[g][i]
                for j in range(a, b):
                    last = nc.vector.tensor_scalar(y[:, g, j], v2[:, g, j], mv2[:, g, j, 0:1], rstd2[:, g, j:j + 1],
                                                   ALU.subtract, ALU.mult)
                last.then_inc(y_ready[g][i], 1)

            def scales_of_w1():
                dve.wait_ge(w1_in, 16)
                nc.vector.tensor_reduce(sum1[:], w1_sb[:], AX_X, ALU.add,
                                        apply_absolute_value=True).then_inc(sum1_ready, 1)
                dve.wait_ge(sum1_ready, 1)
                nc.vector.tensor_scalar(alpha1[:], sum1[:], 1.0 / D, None, ALU.mult).then_inc(alpha1_ready, 1)

            def sums_of_w2():
                dve.wait_ge(w2_in, 16)
                nc.vector.tensor_reduce(sum2[:], w2_sb[:], AX_X, ALU.add,
                                        apply_absolute_value=True).then_inc(sum2_ready, 1)
                dve.wait_ge(ident_ready, 1)
                dve.wait_ge(sum2_ready, 1)
                nc.vector.tensor_scalar(diag2[:], ident[:], sum2[:, 0:1], None, ALU.mult).then_inc(diag2_ready, 1)

            def binarise_w2():
                n = unit("a", 0)
                dve.wait_ge(rows_ready, n + 1)
                dve.wait_ge(sign2_ready, 1)
                nc.vector.scalar_tensor_tensor(out=bw2T[:], in0=sign2[:], scalar=1.0 / H,
                                               in1=rows[n % ROW_BANKS][:, 0:1].to_broadcast([P, HC, D]),
                                               op0=ALU.mult, op1=ALU.mult).then_inc(rows_taken, 1)

            mean_squares(0, 0, 2)
            mean_squares(0, 2, 4)
            scale_rows(0, 0, 2)
            scale_rows(0, 2, 4)
            win_low()
            mean_squares(1)
            dve.wait_ge(wnorm_in, 16)
            norm_weight_low_first(0)
            norm_weight_low_first(1)
            scale_rows(1)
            mean_squares(3)
            scale_rows(2)
            norm_weight_low(1)
            scales_of_w1()
            sums_of_w2()
            lambdas(0, 0)
            norm_weight_low(2)
            drive(0, 0)
            wdt_low()
            scan(0, 0)
            drive(0, 1)
            scan(0, 1)
            u_low(2, 0)
            gate_out(0)
            drive(1, 0)
            u_low(2, 1)
            scan(1, 0)
            drive(1, 1)
            norm_weight_low(3)
            scan(1, 1)
            residual1(0)
            gate_out(1)
            u_low(3, 0)
            drive(2, 0)
            u_low(3, 1)
            scan(2, 0)
            residual1(1)
            x1_lo(0)
            drive(2, 1)
            drive(3, 0)
            scan(2, 1)
            layernorm1(1, 0)
            gate_out(2)
            binarise_w2()
            scan(3, 0)
            x1_lo(1)
            residual1(2)
            drive(3, 1)
            dve.wait_ge(b2_in, 16)
            add_b2(0)
            scan(3, 1)
            gate_out(3)
            residual2(0, 0)
            x1_lo(2)
            add_b2(1)
            residual1(3)
            add_b2(2)
            layernorm1(3, 0)
            layernorm1(3, 1)
            x1_lo(3)
            residual2(1, 0)
            residual2(2, 0)
            add_b2(3)
            residual2(2, 1)
            layernorm2(2, 0)
            residual2(3, 0)
            residual2(3, 1)
            residual2(3, 2)
            layernorm2(3, 0)
            layernorm2(3, 1)
            layernorm2(3, 2)


def kernel(L0_attn_x, L0_attn_w_norm, L0_attn_W_in, L0_attn_W_dt, L0_attn_b_dt, L0_attn_W_out,
           L0_ffn_w1, L0_ffn_b1, L0_ffn_w2, L0_ffn_b2):
    import numpy as _np
    import concourse.bacc as _bacc
    from concourse import mybir as _mybir
    from concourse.bass_utils import run_bass_kernel_spmd as _run

    def columns(v):
        return _np.asarray(v).reshape(-1, P).T

    shape = _np.asarray(L0_attn_x).shape
    laid_out = {
        "x": _np.asarray(L0_attn_x).reshape(-1, shape[-1]),
        "w_norm": columns(L0_attn_w_norm),
        "W_inT": _np.asarray(L0_attn_W_in).T,
        "W_dtT": _np.asarray(L0_attn_W_dt).T,
        "b_dt": columns(L0_attn_b_dt),
        "W_outT": _np.asarray(L0_attn_W_out).T,
        "w1": _np.asarray(L0_ffn_w1),
        "w1T": _np.asarray(L0_ffn_w1).T,
        "b1": columns(L0_ffn_b1),
        "w2": _np.asarray(L0_ffn_w2),
        "w2T": _np.asarray(L0_ffn_w2).T,
        "b2": _np.asarray(L0_ffn_b2).reshape(1, -1),
    }
    nc = _bacc.Bacc("TRN2", target_bir_lowering=False, num_devices=1)
    arrays, args = {}, []
    for name, a in laid_out.items():
        a = _np.ascontiguousarray(a)
        arrays[f"in_{name}"] = a
        args.append(nc.dram_tensor(f"in_{name}", a.shape, _mybir.dt.from_np(a.dtype), kind="ExternalInput").ap())
    args.append(nc.dram_tensor("out_y", laid_out["x"].shape, _mybir.dt.float32, kind="ExternalOutput").ap())
    gated_scan_then_binary_ffn(nc, *args)
    r = _run(nc, [arrays], core_ids=[0])
    return r.results[0]["out_y"].reshape(shape)
```
